# Optimizing a Trainium2 kernel written in Bass

```python
import numpy as np
import jax
import jax.numpy as jnp

def _softmax(x, axis=-1):
    return jax.nn.softmax(x, axis=axis)

def _gelu(x):
    return jax.nn.gelu(x, approximate=True)

def _silu(x):
    return jax.nn.silu(x)

def _sigmoid(x):
    return jax.nn.sigmoid(x)

def _layernorm(x, axis=-1, eps=1e-05):
    m = jnp.mean(x, axis=axis, keepdims=True)
    v = jnp.var(x, axis=axis, keepdims=True)
    return (x - m) / jnp.sqrt(v + eps)

def _scatter_add(tgt, idx, src, axis=0):
    return tgt.at[idx].add(src)

def _segment_sum(src, seg, n):
    return jax.ops.segment_sum(src, seg, n)
kernel_name = 'mk_seq_postln_d1_jaxref_r4_444ed0'

def setup_inputs(seed: int=0):
    np.random.seed(seed)
    _w = jnp.asarray

    def _L0_attn_setup():
        import jax, jax.numpy as jnp
        import numpy as np
        STAGES = 3
        CAUSAL = True

        def sine_positional_encoding(T, D, dtype=jnp.float32):
            pos = jnp.arange(T, dtype=dtype)[:, None]
            i = jnp.arange(D)[None, :]
            angle = pos / jnp.power(jnp.asarray(10000.0, dtype), (2 * (i // 2)).astype(dtype) / D)
            return jnp.where(i % 2 == 0, jnp.sin(angle), jnp.cos(angle))
        key = jax.random.key(seed)
        kX, kWp, kbp, kWf, kbf = jax.random.split(key, 5)
        B, T, D = (4, 1024, 256)
        X = jax.random.normal(kX, (B, T, D), dtype=jnp.float32)
        Wp = jax.random.normal(kWp, (D, (STAGES + 1) * D), dtype=jnp.float32) / np.sqrt(D)
        bp = jnp.zeros(((STAGES + 1) * D,), dtype=jnp.float32)
        Wf = jax.random.normal(kWf, (D, STAGES * D), dtype=jnp.float32) / np.sqrt(D)
        bf = jnp.zeros((STAGES * D,), dtype=jnp.float32)
        return {'X': X, 'Wp': Wp, 'bp': bp, 'Wf': Wf, 'bf': bf}
    _L0_attn_in = _L0_attn_setup()

    def _L0_ffn_setup():
        import jax, jax.numpy as jnp
        import numpy as np
        DIM = 256
        HIDDEN = 768
        SCALE = 1.0 / 127.0

        def _dequant(w_int, dtype):
            return w_int.astype(dtype) * jnp.asarray(SCALE, dtype)
        key = jax.random.key(seed)
        k_x, k_g, k_u, k_d = jax.random.split(key, 4)
        x = jax.random.normal(k_x, (4, 512, DIM), dtype=jnp.float32)
        w_gate = jax.random.randint(k_g, (HIDDEN, DIM), -127, 128, dtype=jnp.int32)
        w_up = jax.random.randint(k_u, (HIDDEN, DIM), -127, 128, dtype=jnp.int32)
        w_down = jax.random.randint(k_d, (DIM, HIDDEN), -127, 128, dtype=jnp.int32)
        return {'x': x, 'w_gate': w_gate, 'w_up': w_up, 'w_down': w_down}
    _L0_ffn_in = _L0_ffn_setup()
    _d = {'L0_attn_X': _L0_attn_in['X'], 'L0_attn_Wp': _L0_attn_in['Wp'], 'L0_attn_bp': _L0_attn_in['bp'], 'L0_attn_Wf': _L0_attn_in['Wf'], 'L0_attn_bf': _L0_attn_in['bf'], 'L0_ffn_w_gate': _L0_ffn_in['w_gate'], 'L0_ffn_w_up': _L0_ffn_in['w_up'], 'L0_ffn_w_down': _L0_ffn_in['w_down']}
    _x0 = _d['L0_attn_X']
    _d['L0_attn_X'] = jax.random.normal(jax.random.fold_in(jax.random.key(seed), 1), (4, 2048, 256), dtype=_x0.dtype)
    del _x0
    return _d

def reference(L0_attn_X, L0_attn_Wp, L0_attn_bp, L0_attn_Wf, L0_attn_bf, L0_ffn_w_gate, L0_ffn_w_up, L0_ffn_w_down):

    def _L0_attn_ref(X, Wp, bp, Wf, bf):
        import jax, jax.numpy as jnp
        import numpy as np
        STAGES = 3
        CAUSAL = True

        def sine_positional_encoding(T, D, dtype=jnp.float32):
            pos = jnp.arange(T, dtype=dtype)[:, None]
            i = jnp.arange(D)[None, :]
            angle = pos / jnp.power(jnp.asarray(10000.0, dtype), (2 * (i // 2)).astype(dtype) / D)
            return jnp.where(i % 2 == 0, jnp.sin(angle), jnp.cos(angle))
        B, T, D = X.shape
        xp = (jnp.einsum('btd,de->bte', X, Wp) + bp).reshape(B, T, STAGES + 1, D)
        pos = sine_positional_encoding(T, D, X.dtype)
        f = (pos @ Wf + bf).reshape(T, STAGES, D)
        if CAUSAL:
            xp = jnp.concatenate([xp, jnp.zeros_like(xp)], axis=1)
            f = jnp.concatenate([f, jnp.zeros_like(f)], axis=0)
        L = xp.shape[1]
        F = jnp.fft.rfft(f, axis=0)
        y = xp[:, :, 0, :]
        for i in range(STAGES):
            conv = jnp.fft.irfft(jnp.fft.rfft(y, axis=1) * F[None, :, i, :], n=L, axis=1)
            y = conv * xp[:, :, i + 1, :]
        return y[:, :T, :] if CAUSAL else y

    def _L0_ffn_ref(x, w_gate, w_up, w_down):
        import jax, jax.numpy as jnp
        import numpy as np
        DIM = 256
        HIDDEN = 768
        SCALE = 1.0 / 127.0

        def _dequant(w_int, dtype):
            return w_int.astype(dtype) * jnp.asarray(SCALE, dtype)
        wg = _dequant(w_gate, x.dtype)
        wu = _dequant(w_up, x.dtype)
        wd = _dequant(w_down, x.dtype)
        gate = jnp.einsum('bsd,hd->bsh', x, wg)
        up = jnp.einsum('bsd,hd->bsh', x, wu)
        h = jax.nn.silu(gate) * up
        return jnp.einsum('bsh,dh->bsd', h, wd)
    x = L0_attn_X
    x = _layernorm(x + _L0_attn_ref(x, L0_attn_Wp, L0_attn_bp, L0_attn_Wf, L0_attn_bf), axis=-1)
    x = _layernorm(x + _L0_ffn_ref(x, L0_ffn_w_gate, L0_ffn_w_up, L0_ffn_w_down), axis=-1)
    return x

_drawn_inputs = setup_inputs


def setup_inputs(seed=0):
    import zlib

    import numpy as np

    out = dict(_drawn_inputs(seed))
    spreads = {'L0_attn_bp': (0.0, 0.1), 'L0_attn_bf': (0.0, 0.1)}
    factors = {}
    for name, (base, spread) in spreads.items():
        noise = np.random.default_rng([zlib.crc32(name.encode()), seed]).standard_normal(out[name].shape)
        drawn = base * np.exp(spread * noise) if base else spread * noise
        out[name] = jnp.asarray(drawn.astype(out[name].dtype))
    for name, factor in factors.items():
        out[name] = (out[name] * factor).astype(out[name].dtype)
    return out
```

```python
from contextlib import ExitStack

import numpy as np

import concourse.bass as bass
from concourse import mybir

F32 = mybir.dt.float32
F16 = mybir.dt.float16
I32 = mybir.dt.int32
ALU = mybir.AluOpType
ACT = mybir.ActivationFunctionType
AX_X = mybir.AxisListType.X

P = 128
NB, T, D = 4, 2048, 256
NS = 3
NA = T // P
NG, CG = 4, 64
NSUB, CS = 4, 16
W = NB * CG
SW = NB * CS
KT = D // P
NL = 2 * P
HID = 768
HM = HID // P
NTOK = NB * P
EPS = 1e-5
BSC = 2.0 ** -3
XS = 2.0 ** 10
HS = 2.0 ** -2
QS = 1.0 / 127.0


def program(nc, XT, X, WPG, BPG, WF, BFC, BFR, POSR, EF, EI, STEP, SEL, FLIP, ONES, IDENT, WGT, WUT, WDT, OUT):
    fscr = nc.dram_tensor("filter_rows", [NS * D, NL * 2], F16)
    y3scr = nc.dram_tensor("attn_out", [NG, P, NA * W], F32)
    fscr_ap, y3_ap = fscr.ap(), y3scr.ap()

    with ExitStack() as ctx:
        def sb(name, shape, dt=F32):
            return ctx.enter_context(nc.sbuf_tensor(name, shape, dt))

        def sem(name):
            return ctx.enter_context(nc.semaphore(name))

        def psum(name):
            return ctx.enter_context(nc.psum_tensor(name, [P, 512], F32))

        xp = sb("xp", [P, NA, NS + 1, W])
        yh = sb("yh", [P, NA, W], F16)
        yl = sb("yl", [P, NA, W], F16)
        toep = sb("toep", [P, NSUB, CS, 2 * P], F16)
        ef = sb("ef", [P, NA - 1, 4, P], F16)
        ei = sb("ei", [P, 2, T])
        step = sb("step", [P, NA - 1, P], F16)
        sel = sb("sel", [P, NA, P], F16)
        flip = sb("flip", [P, P], F16)
        wf = sb("wf", [P, 2, NS * D])
        wp = sb("wp", [P, KT, NG, (NS + 1) * CG])
        bp = sb("bp", [P, NG, (NS + 1) * CG])
        bfr = sb("bfr", [P, NS * D])
        bfc = sb("bfc", [P, NS * D // P])
        xt = sb("xt", [P, 2, KT, NB, P])
        prod = sb("prod", [P, 2, 2, 2 * W])
        gz = sb("gz", [P, 3, 2, W])
        pv = sb("pv", [P, W])
        pb = sb("pb", [P, W], F16)
        junk = sb("junk", [P, 4, W], F16)
        nrm = sb("nrm", [P, 4])
        nsum = sb("nsum", [P, 1])
        ebits = sb("ebits", [P, 1], I32)
        scl = sb("scl", [P, 1], I32)
        iscl = sb("iscl", [P, 1], I32)
        ones = sb("ones", [P, P])
        posr = xt[:, 0]
        frow = xp[:, 0:3].rearrange("p a s w -> p (a s w)").bitcast(F16)[:, 0:6 * 2 * NL].rearrange(
            "p (m l h) -> p m l h", m=6, h=2)
        ftmp = xp[:, 4, 0:3].rearrange("p s w -> p (s w)")

        bank = [psum(f"bank{i}") for i in range(8)]
        b_state, b_copy, b_pre = bank[4], bank[5:7], bank[7]
        dsum = xp[:, :, 0, :].bitcast(F16).rearrange("p a (u h w) -> p a u h w", u=NSUB, h=2)
        scale = scl[:, 0:1].bitcast(F32)
        unscale = iscl[:, 0:1].bitcast(F32)

        s_const = sem("s_const")
        s_wf = sem("s_wf")
        s_tab = sem("s_tab")
        f_done = sem("f_done")
        f_zero = sem("f_zero")
        f_tmp = sem("f_tmp")
        f_hi = sem("f_hi")
        f_rows = sem("f_rows")
        f_stored = sem("f_stored")
        xt_in = [sem(f"xt_in{k}") for k in range(2)]
        toep_in = [sem(f"toep_in{k}") for k in range(NSUB)]
        proj_done = sem("proj_done")
        proj_used = sem("proj_used")
        nrm_part = sem("nrm_part")
        nrm_ready = sem("nrm_ready")
        norm_done = sem("norm_done")
        ebits_ready = sem("ebits_ready")
        scale_ready = sem("scale_ready")
        yh_ready = sem("yh_ready")
        yl_ready = sem("yl_ready")
        toep_done = sem("toep_done")
        toep_high = sem("toep_high")
        toep_low = sem("toep_low")
        pre_done = sem("pre_done")
        pv_ready = sem("pv_ready")
        pb_hi = sem("pb_hi")
        pb_ready = sem("pb_ready")
        st_done = sem("st_done")
        st_copied = sem("st_copied")
        mult_done = sem("mult_done")
        gz_ready = sem("gz_ready")
        inv_done = sem("inv_done")
        gated = sem("gated")
        y3_out = sem("y3_out")

        block = ctx.enter_context(nc.Block())

        @block.sync
        def _(sp):
            sp.dma_start(wf[:], WF).then_inc(s_wf, 16)
            sp.dma_start(posr[:, 0, 0:2, :], POSR).then_inc(s_wf, 16)
            sp.dma_start(bfc[:], BFC).then_inc(s_wf, 16)
            sp.dma_start(wp[:], WPG).then_inc(s_const, 16)
            sp.dma_start(bp[:], BPG.partition_broadcast(P)).then_inc(s_const, 16)
            sp.dma_start(ones[:], ONES).then_inc(s_const, 16)
            sp.wait_ge(f_done, 6)
            sp.wait_ge(f_rows, 6)
            for m in range(6):
                sp.dma_start(fscr_ap[m * P:(m + 1) * P, :], frow[:, m].rearrange(
                    "p l h -> p (l h)")).then_inc(f_stored, 16)
            sp.dma_start(bfr[:], BFR.partition_broadcast(P)).then_inc(s_tab, 16)
            sp.dma_start(step[:], STEP).then_inc(s_tab, 16)
            sp.dma_start(sel[:], SEL).then_inc(s_tab, 16)
            sp.dma_start(flip[:], FLIP).then_inc(s_tab, 16)
            sp.dma_start(ef[:], EF).then_inc(s_tab, 16)
            sp.dma_start(ei[:], EI).then_inc(s_tab, 16)
            sp.wait_ge(f_stored, 6 * 16)
            with sp.Fori(0, NG) as g:
                for a in range(NA):
                    sp.wait_ge(proj_done, g * NA + max(a - 1, 0))
                    sp.dma_start(xt[:, a % 2], XT[:, :, a]).then_inc(xt_in[a % 2], 16)
                with sp.Fori(0, NS) as i:
                    n = g * NS + i
                    for u in range(NSUB):
                        sp.wait_ge(toep_done, n * NSUB)
                        src = bass.AP(tensor=fscr_ap.tensor, offset=(i * D + g * CG + u * CS) * (2 * NL),
                                      ap=[[2, P], [2 * NL, CS], [1, 2 * P]])
                        sp.dma_start(toep[:, u], src).then_inc(toep_in[u], 16)
                sp.wait_ge(gated, (g + 1) * NS * NA)
                sp.dma_start(y3_ap[bass.ds(g, 1)].rearrange("o p (a w) -> p (o a) w", w=W),
                             xp[:, :, 0]).then_inc(y3_out, 16)
            sp.wait_ge(y3_out, NG * 16)

        @block.tensor
        def _(pe):
            pe.wait_ge(s_wf, 48)
            for m in range(6):
                for h in range(2):
                    mm = pe.matmul(bank[m][:, 0:P], wf[:, h, m * P:(m + 1) * P],
                                   posr[:, 0, h, :], start=(h == 0), stop=(h == 1))
                mm.then_inc(f_done, 1)
            pe.wait_ge(s_const, 48)
            pe.wait_ge(f_tmp, 6)
            with pe.Fori(0, NG) as g:
                for a in range(NA):
                    pe.wait_ge(proj_used, g * NA + max(a - 1, 0))
                    if a == 0:
                        pe.wait_ge(gated, g * NS * NA)
                    pe.wait_ge(xt_in[a % 2], g * (NA // 2 * 16) + (a // 2 + 1) * 16)
                    for b in range(NB):
                        for k in range(KT):
                            mm = pe.matmul(bank[2 * (a % 2) + b // 2][:, (b % 2) * W:(b % 2 + 1) * W],
                                           xt[:, a % 2, k, b, :], wp[:, k, bass.ds(g, 1), :],
                                           start=(k == 0), stop=(k == KT - 1))
                    mm.then_inc(proj_done, 1)
                with pe.Fori(0, NS) as i:
                    n = g * NS + i
                    pe.wait_ge(nrm_ready, n + 1)
                    pe.matmul(b_pre[:, 0:1], ones[:], nsum[:], start=True, stop=True).then_inc(norm_done, 1)
                    for u in range(NSUB):
                        pe.wait_ge(toep_in[u], n * 16 + 16)
                        pe.wait_ge(yh_ready, n * NSUB + u + 1)
                        pe.wait_ge(yl_ready, n * NSUB + u + 1)
                        if u >= 2:
                            pe.wait_ge(toep_low, n * NSUB + u - 1)
                        for c in range(CS):
                            lag = toep[:, u, c, :].rearrange("p (t h) -> p h t", h=2)
                            cols = slice((u * CS + c) * NB, (u * CS + c + 1) * NB)
                            dst = bank[2 * (u % 2) + c // 8][:, (c % 8) * 64:(c % 8 + 1) * 64]
                            pe.matmul(dst, lag[:, 0], yh[:, :, cols], start=True, stop=False)
                            pe.matmul(dst, lag[:, 0], yl[:, :, cols], start=False, stop=False)
                            mm = pe.matmul(dst, lag[:, 1], yh[:, :, cols], start=False, stop=True)
                        mm.then_inc(toep_done, 1)
                    pe.wait_ge(s_tab, 96)
                    for a in range(NA - 1):
                        for y in (yh, yl):
                            mm = pe.matmul(b_pre[:, 0:W], step[:, a, :], y[:, a, :],
                                           start=(a == 0 and y is yh), stop=(a == NA - 2 and y is yl))
                    mm.then_inc(pre_done, 1)
                    for k in range(NA + 1):
                        if k < NA - 1:
                            pe.wait_ge(st_copied, n * (NA - 1) + k)
                            for q, (e, y) in enumerate(((0, yh), (0, yl), (2, yh))):
                                for h in range(2):
                                    mm = pe.matmul(b_state[:, h * W:(h + 1) * W], ef[:, k, e + h, :], y[:, k, :],
                                                   start=(k == 0 and q == 0 and h == 0),
                                                   stop=(k == NA - 2 and q == 2), skip_group_check=True)
                            mm.then_inc(st_done, 1)
                        if k >= 1:
                            a = k - 1
                            dst = bank[a % 2][:, 0:W]
                            if a <= 1:
                                pe.wait_ge(toep_low, n * NSUB + NSUB)
                            else:
                                pe.wait_ge(gated, n * NA + a - 1)
                            for h in range(2):
                                mm = pe.matmul(dst, flip[:], dsum[:, a, :, h, :],
                                               start=(h == 0), stop=(h == 1 and a == 0))
                            if a >= 1:
                                if a == 1:
                                    pe.wait_ge(pb_ready, n + 1)
                                pe.matmul(dst, sel[:, a, :], pb[:], start=False, stop=False)
                                pe.wait_ge(gz_ready, n * (NA - 1) + a)
                                for h in range(2):
                                    mm = pe.matmul(dst, ei[:, h, a * P:(a + 1) * P], gz[:, (a - 1) % 3, h, :],
                                                   start=False, stop=(h == 1))
                            mm.then_inc(inv_done, 1)

        @block.scalar
        def _(act):
            for m in range(6):
                act.wait_ge(f_tmp, m + 1)
                act.wait_ge(f_zero, 1)
                nc.scalar.activation(frow[:, m, 0:P, 0], ftmp[:, m * P:(m + 1) * P],
                                     ACT.Copy).then_inc(f_hi, 1)

            def square(seg, before):
                act.wait_ge(nrm_part, before)
                nc.scalar.activation(junk[:], xp[:, 4 * seg:4 * seg + 4, 0, :], ACT.Square,
                                     accum_out=nrm[:, seg:seg + 1]).then_inc(nrm_part, 1)

            with act.Fori(0, NG) as g:
                for seg in range(4):
                    act.wait_ge(proj_used, g * NA + 4 * seg + 4)
                    square(seg, g * (4 * (NS + 1)) + seg)
                with act.Fori(0, NS) as i:
                    n = g * NS + i
                    act.wait_ge(scale_ready, n + 1)
                    for u in range(NSUB):
                        nc.scalar.activation(yh[:, :, u * SW:(u + 1) * SW], xp[:, :, 0, u * SW:(u + 1) * SW],
                                             ACT.Copy, scale=scale).then_inc(yh_ready, 1)
                    for u in range(NSUB):
                        act.wait_ge(toep_done, n * NSUB + u + 1)
                        for h in range(2):
                            cols = slice(h * SW // 2, (h + 1) * SW // 2)
                            last = nc.scalar.activation(
                                dsum[:, :, u, 0, cols].rearrange("p a (c b) -> p c a b", b=NB),
                                bank[2 * (u % 2) + h][:, :].rearrange("p (c a b) -> p c a b", c=8, b=NB), ACT.Copy)
                        last.then_inc(toep_high, 1)
                    act.wait_ge(pv_ready, n + 1)
                    nc.scalar.activation(pb[:], pv[:], ACT.Copy).then_inc(pb_hi, 1)
                    for k in range(NA - 1):
                        act.wait_ge(st_done, n * (NA - 1) + k + 1)
                        act.wait_ge(mult_done, n * (NA - 1) + max(k - 1, 0))
                        nc.scalar.copy(b_copy[k % 2][:, :], b_state[:, :]).then_inc(st_copied, 1)
                        if k in (7, 11):
                            act.wait_ge(gated, n * NA + k - 3)
                            square((k - 7) // 4, g * (4 * (NS + 1)) + i * 4 + 4 + (k - 7) // 4)
                    for seg in (2, 3):
                        act.wait_ge(gated, n * NA + 4 * seg + 4)
                        square(seg, g * (4 * (NS + 1)) + i * 4 + 4 + seg)

        @block.vector
        def _(dve):
            nc.vector.memset(frow[:, :, P:NL, :], 0.0).then_inc(f_zero, 1)
            dve.wait_ge(s_wf, 48)
            for m in range(6):
                dve.wait_ge(f_done, m + 1)
                nc.vector.tensor_scalar(ftmp[:, m * P:(m + 1) * P], bank[m][:, 0:P],
                                        bfc[:, m:m + 1], None, ALU.add).then_inc(f_tmp, 1)
            for m in range(6):
                dve.wait_ge(f_hi, m + 1)
                nc.vector.tensor_tensor(frow[:, m, 0:P, 1], ftmp[:, m * P:(m + 1) * P],
                                        frow[:, m, 0:P, 0], ALU.subtract).then_inc(f_rows, 1)
            dve.wait_ge(f_stored, 6 * 16)
            dve.wait_ge(s_const, 48)
            with dve.Fori(0, NG) as g:
                dve.wait_ge(y3_out, g * 16)
                dve.wait_ge(nrm_part, g * (4 * (NS + 1)))
                for a in range(NA):
                    dve.wait_ge(proj_done, g * NA + a + 1)
                    for h in range(2):
                        last = nc.vector.tensor_tensor(
                            xp[:, a].rearrange("p s (c b) -> p (s c) b", b=NB)[:, :, 2 * h:2 * h + 2],
                            bank[2 * (a % 2) + h][:, :].rearrange("p (b c) -> p c b", b=2),
                            bp[:, bass.ds(g, 1), :].rearrange("p o c -> p (o c)").unsqueeze(2).broadcast_to(
                                [P, (NS + 1) * CG, 2]), ALU.add)
                    last.then_inc(proj_used, 1)
                with dve.Fori(0, NS) as i:
                    n = g * NS + i
                    dve.wait_ge(nrm_part, g * (4 * (NS + 1)) + i * 4 + 4)
                    nc.vector.tensor_reduce(nsum[:], nrm[:], AX_X, ALU.add).then_inc(nrm_ready, 1)
                    dve.wait_ge(norm_done, n + 1)
                    nc.vector.tensor_scalar(ebits[:], b_pre[:, 0:1].bitcast(I32), 24, None,
                                            ALU.logical_shift_right).then_inc(ebits_ready, 1)
                    dve.wait_ge(ebits_ready, n + 1)
                    nc.vector.tensor_scalar(scl[:], ebits[:], -float(1 << 23), float(199 << 23), ALU.mult, ALU.add)
                    nc.vector.tensor_scalar(iscl[:], ebits[:], float(1 << 23), float(55 << 23), ALU.mult,
                                            ALU.add).then_inc(scale_ready, 1)
                    dve.wait_ge(scale_ready, n + 1)
                    for u in range(NSUB):
                        dve.wait_ge(yh_ready, n * NSUB + u + 1)
                        nc.vector.scalar_tensor_tensor(
                            out=yl[:, :, u * SW:(u + 1) * SW], in0=xp[:, :, 0, u * SW:(u + 1) * SW], scalar=scale,
                            in1=yh[:, :, u * SW:(u + 1) * SW], op0=ALU.mult, op1=ALU.subtract).then_inc(yl_ready, 1)

                    def spread(t, rep):
                        v = t.unsqueeze(1).unsqueeze(3).broadcast_to([P, rep, CG, NB])
                        return v

                    for u in range(NSUB):
                        dve.wait_ge(toep_high, n * NSUB + u + 1)
                        for h in range(2):
                            cols = slice(h * SW // 2, (h + 1) * SW // 2)
                            last = nc.vector.tensor_tensor(
                                dsum[:, :, u, 1, cols].rearrange("p a (c b) -> p c a b", b=NB),
                                bank[2 * (u % 2) + h][:, :].rearrange("p (c a b) -> p c a b", c=8, b=NB),
                                dsum[:, :, u, 0, cols].rearrange("p a (c b) -> p c a b", b=NB), ALU.subtract)
                        last.then_inc(toep_low, 1)
                    dve.wait_ge(s_tab, 96)
                    dve.wait_ge(pre_done, n + 1)
                    nc.vector.scalar_tensor_tensor(
                        out=pv[:].rearrange("p (c b) -> p c b", b=NB),
                        in0=b_pre[:, 0:W].rearrange("p (c b) -> p c b", b=NB), scalar=BSC,
                        in1=bfr[:, bass.ds(i * D + g * CG, CG)].unsqueeze(2).broadcast_to([P, CG, NB]),
                        op0=ALU.mult, op1=ALU.mult).then_inc(pv_ready, 1)
                    for k in range(NA + 1):
                        if k < NA - 1:
                            dve.wait_ge(st_copied, n * (NA - 1) + k + 1)
                            dve.wait_ge(gz_ready, n * (NA - 1) + max(k - 1, 0))
                            for h in range(2):
                                last = nc.vector.tensor_tensor(
                                    prod[:, k % 2, h].rearrange("p (r c b) -> p r c b", r=2, b=NB),
                                    b_copy[k % 2][:, :].rearrange("p (r c b) -> p r c b", r=2, b=NB),
                                    spread(wf[:, h, bass.ds(i * D + g * CG, CG)], 2), ALU.mult)
                            last.then_inc(mult_done, 1)
                        if k == 0:
                            dve.wait_ge(pb_hi, n + 1)
                            nc.vector.tensor_tensor(pb[32:64, :], pv[32:64, :], pb[32:64, :],
                                                    ALU.subtract).then_inc(pb_ready, 1)
                        if k >= 1:
                            a = k - 1
                            dve.wait_ge(inv_done, n * NA + a + 1)
                            nc.vector.scalar_tensor_tensor(
                                out=xp[:, a, 0, :], in0=bank[a % 2][:, 0:W], scalar=unscale,
                                in1=xp[:, a, bass.ds(i + 1, 1), :].rearrange("p o w -> p (o w)"),
                                op0=ALU.mult, op1=ALU.mult).then_inc(gated, 1)

        @block.gpsimd
        def _(pool):
            with pool.Fori(0, NG) as g:
                with pool.Fori(0, NS) as i:
                    n = g * NS + i
                    for k in range(NA - 1):
                        pool.wait_ge(mult_done, n * (NA - 1) + k + 1)
                        pool.wait_ge(inv_done, n * NA + max(k - 1, 0))
                        pa, pbt = prod[:, k % 2, 0], prod[:, k % 2, 1]
                        nc.gpsimd.tensor_tensor(gz[:, k % 3, 0], pa[:, 0:W], pbt[:, W:2 * W], ALU.add)
                        nc.gpsimd.tensor_tensor(gz[:, k % 3, 1], pbt[:, 0:W], pa[:, W:2 * W],
                                                ALU.subtract).then_inc(gz_ready, 1)

    with ExitStack() as ctx:
        def sb(name, shape, dt=F32):
            return ctx.enter_context(nc.sbuf_tensor(name, shape, dt))

        def sem(name):
            return ctx.enter_context(nc.semaphore(name))

        def psum(name):
            return ctx.enter_context(nc.psum_tensor(name, [P, 512], F32))

        ident = sb("ident", [P, P])
        wi = sb("wi", [P, 3, 2 * HID], I32)
        wg = sb("wg", [P, KT, HID], F16)
        wu = sb("wu", [P, KT, HID], F16)
        wd = sb("wd", [P, HM, D], F16)
        ya = sb("ya", [P, 2, NG, W])
        xr = sb("xr", [P, 2, NB, D])
        x1 = sb("x1", [P, 2, NB, D])
        x1n = sb("x1n", [P, 3, NB, D])
        xh = sb("xh", [P, 2, KT, NTOK], F16)
        xl = sb("xl", [P, 2, KT, NTOK], F16)
        sg = sb("sg", [P, 2, NTOK])
        hf = sb("hf", [P, 2, NTOK])
        hh = sb("hh", [P, 2, HM, NTOK], F16)
        hl = sb("hl", [P, 2, HM, NTOK], F16)
        zz = sb("zz", [P, NB, D])
        oo = sb("oo", [P, 2, NB, D])
        st = sb("st", [P, 2, NB, 6])
        mv = sb("mv", [P, 2, NB, 2])
        rs = sb("rs", [P, 2, NB])
        mhalf = sb("mhalf", [P, NB])
        epst = sb("epst", [P, NB])
        tick = sb("tick", [P, 1])
        b_t = [psum(f"bt{k}") for k in range(KT)]
        b_g = [psum(f"bg{k}") for k in range(2)]
        b_u = [psum(f"bu{k}") for k in range(2)]
        b_d = [psum(f"bd{k}") for k in range(2)]

        w_in = sem("w_in")
        w_cast = sem("w_cast")
        ya_in = [sem(f"ya_in{k}") for k in range(2)]
        xr_in = [sem(f"xr_in{k}") for k in range(2)]
        x1_ready = sem("x1_ready")
        stats = sem("stats")
        mean1 = sem("mean1")
        vare = sem("vare")
        rstd = sem("rstd")
        const_ready = sem("const_ready")
        x1n_ready = sem("x1n_ready")
        tr_done = sem("tr_done")
        xh_ready = sem("xh_ready")
        xl_ready = sem("xl_ready")
        g_done = sem("g_done")
        u_done = sem("u_done")
        sg_ready = sem("sg_ready")
        hf_ready = sem("hf_ready")
        hh_ready = sem("hh_ready")
        hl_ready = sem("hl_ready")
        d_done = sem("d_done")
        zz_ready = sem("zz_ready")
        oo_ready = sem("oo_ready")
        out_done = [sem(f"out_done{k}") for k in range(2)]

        block = ctx.enter_context(nc.Block())
        xview = X.rearrange("b (a t) d -> t a b d", t=P)
        oview = OUT.rearrange("b (a t) d -> t a b d", t=P)
        yview = y3_ap.rearrange("g p (a w) -> p a g w", w=W)

        @block.sync
        def _(sp):
            def load(k, par):
                sp.dma_start(ya[:, par], yview[:, bass.ds(k, 1)].rearrange("p o g w -> p (o g) w")).then_inc(ya_in[par], 16)
                sp.dma_start(xr[:, par], xview[:, bass.ds(k, 1)].rearrange("p o b d -> p (o b) d")).then_inc(xr_in[par], 16)

            load(0, 0)
            load(1, 1)
            sp.dma_start(wi[:, 0].rearrange("p (k h) -> p k h", k=KT), WGT).then_inc(w_in, 16)
            sp.dma_start(wi[:, 1].rearrange("p (k h) -> p k h", k=KT), WUT).then_inc(w_in, 16)
            sp.dma_start(wi[:, 2].rearrange("p (k h) -> p k h", k=HM), WDT).then_inc(w_in, 16)
            sp.dma_start(ident[:], IDENT).then_inc(w_in, 16)

            def store(k, par):
                sp.wait_ge(oo_ready, k * NB + NB)
                sp.dma_start(oview[:, bass.ds(k, 1)].rearrange("p o b d -> p (o b) d"), oo[:, par]).then_inc(out_done[par], 16)

            with sp.Fori(0, NA // 2 - 1) as kk:
                for par in range(2):
                    k = kk * 2 + par
                    sp.wait_ge(x1_ready, k + 1)
                    load(k + 2, par)
                    store(k, par)
            store(NA - 2, 0)
            store(NA - 1, 1)
            sp.wait_ge(out_done[0], NA // 2 * 16)
            sp.wait_ge(out_done[1], NA // 2 * 16)

        @block.tensor
        def _(pe):
            def transposes(k, par):
                pe.wait_ge(x1n_ready, k * NB + NB)
                pe.wait_ge(xl_ready, k * KT)
                for t in range(KT):
                    for b in range(NB):
                        mm = pe.transpose(b_t[t][:, b * P:(b + 1) * P], x1n[:, par, b, t * P:(t + 1) * P], ident[:])
                    mm.then_inc(tr_done, 1)

            def gate_up(k, par):
                pe.wait_ge(xh_ready, k * KT + KT)
                pe.wait_ge(xl_ready, k * KT + KT)
                for m in range(HM):
                    for wt, bk, free, done in ((wg, b_g, sg_ready, g_done), (wu, b_u, hf_ready, u_done)):
                        pe.wait_ge(free, k * HM + m - 1 if m >= 2 else k * HM)
                        for t in range(KT):
                            for y in (xh, xl):
                                mm = pe.matmul(bk[m % 2][:, :], wt[:, t, m * P:(m + 1) * P], y[:, par, t, :],
                                               start=(t == 0 and y is xh), stop=(t == KT - 1 and y is xl))
                        mm.then_inc(done, 1)

            def down(k, par):
                pe.wait_ge(hh_ready, k * HM + HM)
                pe.wait_ge(hl_ready, k * HM + HM)
                pe.wait_ge(zz_ready, k * 2)
                for b in range(NB):
                    for m in range(HM):
                        for h in (hh, hl):
                            mm = pe.matmul(b_d[b // 2][:, (b % 2) * D:(b % 2 + 1) * D],
                                           h[:, par, m, b * P:(b + 1) * P], wd[:, m, :],
                                           start=(m == 0 and h is hh), stop=(m == HM - 1 and h is hl))
                    if b % 2:
                        mm.then_inc(d_done, 1)

            pe.wait_ge(w_in, 64)
            pe.wait_ge(w_cast, 3)
            transposes(0, 0)
            gate_up(0, 0)
            transposes(1, 1)
            with pe.Fori(0, 2) as q:
                for r in range(6):
                    k = q * 6 + (r + 1)
                    gate_up(k, (r + 1) % 2)
                    transposes(k + 1, (r + 2) % 3)
                    down(k - 1, r % 2)
            for k in range(13, NA):
                gate_up(k, k % 2)
                if k + 1 < NA:
                    transposes(k + 1, (k + 1) % 3)
                down(k - 1, (k - 1) % 2)
            down(NA - 1, (NA - 1) % 2)

        @block.scalar
        def _(act):
            def split_x(k, par):
                act.wait_ge(tr_done, k * KT + KT)
                for t in range(KT):
                    nc.scalar.activation(xh[:, par, t, :], b_t[t][:, :], ACT.Copy, scale=XS).then_inc(xh_ready, 1)

            def hidden(k, par):
                for m in range(HM + 1):
                    if m < HM:
                        act.wait_ge(g_done, k * HM + m + 1)
                        act.wait_ge(hf_ready, k * HM + m - 1 if m >= 2 else k * HM)
                        nc.scalar.activation(sg[:, m % 2, :], b_g[m % 2][:, :], ACT.Silu,
                                             scale=QS / XS).then_inc(sg_ready, 1)
                    if m >= 1:
                        act.wait_ge(hf_ready, k * HM + m)
                        nc.scalar.activation(hh[:, par, m - 1, :], hf[:, (m - 1) % 2, :], ACT.Copy).then_inc(hh_ready, 1)

            split_x(0, 0)
            hidden(0, 0)
            split_x(1, 1)
            with act.Fori(0, NA // 2 - 1) as kk:
                for r in range(2):
                    k = kk * 2 + (r + 1)
                    hidden(k, (r + 1) % 2)
                    split_x(k + 1, r % 2)
            hidden(NA - 1, (NA - 1) % 2)

        @block.vector
        def _(dve):
            def norm_stats(src, slot, count):
                for b in range(NB):
                    last = nc.vector.bn_stats(st[:, slot, b, :], src[:, b, :])
                last.then_inc(stats, 1)
                dve.wait_ge(stats, count)
                nc.vector.memset(tick[:], 0.0)
                for b in range(NB):
                    last = nc.vector.bn_aggr(mv[:, slot, b, :], st[:, slot, b, :])
                last.then_inc(mean1, 1)

            def scaled(dst, src, slot, b):
                return nc.vector.tensor_scalar(dst[:, b, :], src[:, b, :], mv[:, slot, b, 0:1], rs[:, slot, b:b + 1],
                                               ALU.subtract, ALU.mult)

            def pre(k, par, n_stats):
                dve.wait_ge(ya_in[par], bass_half(k, par))
                dve.wait_ge(xr_in[par], bass_half(k, par))
                nc.vector.tensor_tensor(
                    x1[:, 0].rearrange("p b (g c) -> p b g c", g=NG),
                    ya[:, par].rearrange("p g (c b) -> p b g c", b=NB),
                    xr[:, par].rearrange("p b (g c) -> p b g c", g=NG), ALU.add).then_inc(x1_ready, 1)
                dve.wait_ge(x1_ready, k + 1)
                norm_stats(x1[:, 0], 0, n_stats)

            def bass_half(k, par):
                return (k - par) * 8 + 16

            def norm1(k, slot3, n_stats):
                dve.wait_ge(rstd, n_stats)
                for b in range(NB):
                    scaled(x1n[:, slot3], x1[:, 0], 0, b).then_inc(x1n_ready, 1)

            def split_x(k, par):
                for t in range(KT):
                    dve.wait_ge(xh_ready, k * KT + t + 1)
                    nc.vector.scalar_tensor_tensor(out=xl[:, par, t, :], in0=b_t[t][:, :], scalar=XS,
                                                   in1=xh[:, par, t, :], op0=ALU.mult,
                                                   op1=ALU.subtract).then_inc(xl_ready, 1)

            def product(k, m):
                dve.wait_ge(u_done, k * HM + m + 1)
                dve.wait_ge(sg_ready, k * HM + m + 1)
                dve.wait_ge(hl_ready, k * HM + m - 1 if m >= 2 else k * HM)
                nc.vector.scalar_tensor_tensor(out=hf[:, m % 2, :], in0=b_u[m % 2][:, :], scalar=HS * QS / XS,
                                               in1=sg[:, m % 2, :], op0=ALU.mult,
                                               op1=ALU.mult).then_inc(hf_ready, 1)

            def low(k, m, par):
                dve.wait_ge(hh_ready, k * HM + m + 1)
                nc.vector.tensor_tensor(hl[:, par, m, :], hf[:, m % 2, :], hh[:, par, m, :],
                                        ALU.subtract).then_inc(hl_ready, 1)

            def post_sum(k, slot3, n_stats):
                dve.wait_ge(oo_ready, k * NB)
                for h in range(2):
                    dve.wait_ge(d_done, k * 2 + h + 1)
                    nc.vector.scalar_tensor_tensor(
                        out=zz[:, 2 * h:2 * h + 2, :], in0=b_d[h][:, :].rearrange("p (b c) -> p b c", b=2),
                        scalar=QS / HS, in1=x1n[:, slot3, 2 * h:2 * h + 2, :], op0=ALU.mult,
                        op1=ALU.add).then_inc(zz_ready, 1)
                dve.wait_ge(zz_ready, k * 2 + 2)
                norm_stats(zz, 1, n_stats)

            def post_norm(k, par, n_stats):
                dve.wait_ge(rstd, n_stats)
                for b in range(NB):
                    scaled(oo[:, par], zz, 1, b).then_inc(oo_ready, 1)

            def step_body(k, r2, r3, middle, has_prev, has_next, out_free):
                for m in range(HM):
                    product(k, m)
                    if m >= 1:
                        low(k, m - 1, r2)
                    if m == 1 and has_next:
                        pre(k + 1, 1 - r2, middle)
                    if m == 3 and has_next:
                        norm1(k + 1, (r3 + 1) % 3, middle)
                low(k, HM - 1, r2)
                if has_next:
                    split_x(k + 1, 1 - r2)
                if has_prev:
                    if out_free is not None:
                        dve.wait_ge(out_done[1 - r2], out_free)
                    post_sum(k - 1, (r3 + 2) % 3, middle + 1)
                    post_norm(k - 1, 1 - r2, middle + 1)

            nc.vector.memset(epst[:], EPS)
            nc.vector.memset(mhalf[:], -0.5).then_inc(const_ready, 1)
            pre(0, 0, 1)
            dve.wait_ge(w_in, 64)
            for wt, q in ((wg, 0), (wu, 1), (wd, 2)):
                nc.vector.tensor_copy(wt[:].rearrange("p k h -> p (k h)"), wi[:, q]).then_inc(w_cast, 1)
            norm1(0, 0, 1)
            split_x(0, 0)
            step_body(0, 0, 0, 2, False, True, None)
            with dve.Fori(0, 2) as q:
                for r in range(6):
                    k = q * 6 + (r + 1)
                    step_body(k, (r + 1) % 2, (r + 1) % 3, k * 2 + 1, True, True,
                              (q * 3 + r // 2) * 16)
            for k in range(13, NA):
                if k + 1 < NA:
                    step_body(k, k % 2, k % 3, 2 * k + 1, True, True, (k - 1) // 2 * 16)
                else:
                    step_body(k, k % 2, k % 3, 2 * k, True, False, (k - 1) // 2 * 16)
            k = NA
            dve.wait_ge(out_done[1], (k - 1) // 2 * 16)
            post_sum(k - 1, (k - 1) % 3, 2 * NA)
            post_norm(k - 1, 1, 2 * NA)

        @block.gpsimd
        def _(pool):
            pool.wait_ge(const_ready, 1)

            def root(slot, n):
                pool.wait_ge(mean1, n)
                nc.gpsimd.tensor_tensor(rs[:, slot], mv[:, slot, :, 1], epst[:], ALU.add).then_inc(vare, 1)
                pool.wait_ge(vare, n)
                nc.gpsimd.tensor_tensor(rs[:, slot], rs[:, slot], mhalf[:], ALU.pow).then_inc(rstd, 1)

            root(0, 1)
            root(0, 2)
            with pool.Fori(1, NA - 1) as k:
                root(0, k * 2 + 1)
                root(1, k * 2 + 2)
            root(1, 2 * NA - 1)
            root(1, 2 * NA)


def tables():
    k = np.arange(P)
    period = np.power(np.float32(10000.0), (2 * k).astype(np.float32) / np.float32(D)).astype(np.float32)
    t = np.arange(T)
    lag_angle = (t[:P, None].astype(np.float32) / period[None, :]).astype(np.float32).astype(np.float64)
    angle = t[:, None].astype(np.float64) / period[None, :].astype(np.float64)
    sin, cos = np.sin(angle), np.cos(angle)
    posr = np.stack([np.sin(lag_angle).T, np.cos(lag_angle).T], 1).astype(np.float32)
    high = [x.astype(np.float16) for x in (cos, sin)]
    low = [(x - h.astype(np.float64)).astype(np.float16) for x, h in zip((cos, sin), high)]
    ef = np.stack(high + low, 0).reshape(4, NA, P, P)[:, :NA - 1].transpose(2, 1, 0, 3)
    ei = np.stack([sin.T, cos.T], 1).astype(np.float32)
    row = np.arange(P)
    step = np.zeros((P, NA - 1, P), np.float16)
    sel = np.zeros((P, NA, P), np.float16)
    for a in range(NA):
        if a < NA - 1:
            step[:, a, (row < 64) & (row % 32 < NA) & (row % 32 > a)] = 1
        sel[[a, 32 + a], a, :] = 1 / BSC
    flip = (np.eye(P)[::-1]).astype(np.float16)
    return posr[:, :, ::-1], np.ascontiguousarray(ef), ei, step, sel, flip


def kernel(L0_attn_X, L0_attn_Wp, L0_attn_bp, L0_attn_Wf, L0_attn_bf, L0_ffn_w_gate, L0_ffn_w_up, L0_ffn_w_down):
    import concourse.bacc as bacc
    from concourse.bass_utils import run_bass_kernel_spmd

    X = np.asarray(L0_attn_X)
    posr, ef, ei, step, sel, flip = tables()

    def by_group(w):
        return w.reshape(w.shape[:-1] + (NS + 1, NG, CG)).swapaxes(-3, -2).reshape(w.shape[:-1] + (NG, (NS + 1) * CG))

    wf = np.asarray(L0_attn_Wf)
    bf = np.asarray(L0_attn_bf)
    arrays = {
        "XT": X.reshape(NB, NA, P, KT, P).transpose(4, 3, 1, 0, 2),
        "X": X,
        "WPG": by_group(np.asarray(L0_attn_Wp)).reshape(KT, P, NG, (NS + 1) * CG).transpose(1, 0, 2, 3),
        "BPG": by_group(np.asarray(L0_attn_bp)),
        "WF": np.stack([wf[0::2], wf[1::2]], 1),
        "BFC": bf.reshape(NS * D // P, P).T,
        "BFR": bf,
        "POSR": posr, "EF": ef, "EI": ei, "STEP": step, "SEL": sel, "FLIP": flip,
        "ONES": np.ones((P, P), np.float32), "IDENT": np.eye(P, dtype=np.float32),
        "WGT": np.asarray(L0_ffn_w_gate).T.reshape(KT, P, HID).transpose(1, 0, 2),
        "WUT": np.asarray(L0_ffn_w_up).T.reshape(KT, P, HID).transpose(1, 0, 2),
        "WDT": np.asarray(L0_ffn_w_down).T.reshape(HM, P, D).transpose(1, 0, 2),
    }
    nc = bacc.Bacc("TRN2", target_bir_lowering=False, num_devices=1)
    ins, args = {}, []
    for name, a in arrays.items():
        ins[f"in_{name}"] = np.ascontiguousarray(a)
        args.append(nc.dram_tensor(f"in_{name}", a.shape, mybir.dt.from_np(a.dtype), kind="ExternalInput").ap())
    args.append(nc.dram_tensor("out_x", [NB, T, D], F32, kind="ExternalOutput").ap())
    program(nc, *args)
    r = run_bass_kernel_spmd(nc, [ins], core_ids=[0])
    return r.results[0]["out_x"]
```

```python
from contextlib import ExitStack

import numpy as np

import concourse.bass as bass
from concourse import mybir

F32 = mybir.dt.float32
F16 = mybir.dt.float16
I32 = mybir.dt.int32
ALU = mybir.AluOpType
ACT = mybir.ActivationFunctionType
AX_X = mybir.AxisListType.X

P = 128
SEG = (4, 8, 12, 15, 16)
LAG = 2
NB, T, D = 4, 2048, 256
NS = 3
NA = T // P
NG, CG = 4, 64
NSUB, CS = 4, 16
W = NB * CG
SW = NB * CS
PIECES = ((0, SW // 2), (SW // 2, SW)) + tuple((u * SW, (u + 1) * SW) for u in range(1, NSUB))
KT = D // P
NL = 2 * P
HID = 768
HM = HID // P
NTOK = NB * P
EPS = 1e-5
BSC = 2.0 ** -3
XS = 2.0 ** 10
HS = 2.0 ** -2
QS = 1.0 / 127.0


def program(nc, XT, X, WPG, BPG, WF, BFC, BFR, POSR, EF, EI, STEP, SEL, FLIP, ONES, IDENT, WGT, WUT, WDT, OUT):
    fscr = nc.dram_tensor("filter_rows", [NS * D, NL * 2], F16)
    y3scr = nc.dram_tensor("attn_out", [NG, P, NA * W], F32)
    fscr_ap, y3_ap = fscr.ap(), y3scr.ap()

    whole = ExitStack()
    wg = whole.enter_context(nc.sbuf_tensor("wg", [P, KT, HID], F16))
    wu = whole.enter_context(nc.sbuf_tensor("wu", [P, KT, HID], F16))
    wd = whole.enter_context(nc.sbuf_tensor("wd", [P, HM, D], F16))
    w_in = whole.enter_context(nc.semaphore("w_in"))
    w_cast = whole.enter_context(nc.semaphore("w_cast"))

    with ExitStack() as ctx:
        def sb(name, shape, dt=F32):
            return ctx.enter_context(nc.sbuf_tensor(name, shape, dt))

        def sem(name):
            return ctx.enter_context(nc.semaphore(name))

        def psum(name):
            return ctx.enter_context(nc.psum_tensor(name, [P, 512], F32))

        xp = sb("xp", [P, NA, NS + 1, W])
        yh = sb("yh", [P, NA, W], F16)
        yl = sb("yl", [P, NA, W], F16)
        toep = sb("toep", [P, NSUB, CS, 2 * P], F16)
        ef = sb("ef", [P, NA - 1, 4, P], F16)
        ei = sb("ei", [P, 2, T])
        step = sb("step", [P, NA - 1, P // 2], F16)
        sel = sb("sel", [P, NA, P], F16)
        flip = sb("flip", [P, P], F16)
        wf = sb("wf", [P, 2, NS * D])
        wp = sb("wp", [P, KT, NG, (NS + 1) * CG])
        bp = sb("bp", [P, NG, (NS + 1) * CG])
        bfr = sb("bfr", [P, NS * D])
        bfc = sb("bfc", [P, NS * D // P])
        xt = sb("xt", [P, 2, KT, NB, P])
        prod = sb("prod", [P, 2, 2, 2 * W])
        gz = sb("gz", [P, 3, 2, W])
        pv = sb("pv", [P, W])
        pb = sb("pb", [P, W], F16)
        junk = sb("junk", [P, 4, W], F16)
        nrm = sb("nrm", [P, len(SEG)])
        nsum = sb("nsum", [P, 1])
        ebits = sb("ebits", [P, 1], I32)
        scl = sb("scl", [P, 1], I32)
        iscl = sb("iscl", [P, 1], I32)
        ones = sb("ones", [P, P])
        spare = toep[:].rearrange("p u c l -> p (u c l)")
        posr = spare[:, 0:4 * P].bitcast(F32).rearrange("p (h l) -> p h l", h=2)
        ftmp = spare[:, 4 * P:4 * P + 2 * NS * D].bitcast(F32)
        frow = spare[:, 4 * P + 2 * NS * D:4 * P + 2 * NS * D + 6 * 2 * NL].rearrange("p (m l h) -> p m l h", m=6, h=2)

        wi = xp[:, 10:15].rearrange("p a s w -> p (a s w)").bitcast(I32)[:, 0:6 * HID].rearrange("p (q h) -> p q h", q=3)

        bank = [psum(f"bank{i}") for i in range(8)]
        b_state, b_copy, b_pre = bank[4], bank[5:7], bank[7]
        dsum = xp[:, :, 0, :].bitcast(F16).rearrange("p a (u h w) -> p a u h w", u=NSUB, h=2)
        scale = scl[:, 0:1].bitcast(F32)
        unscale = iscl[:, 0:1].bitcast(F32)

        s_const = sem("s_const")
        s_wf = sem("s_wf")
        s_tab = sem("s_tab")
        f_done = sem("f_done")
        f_zero = sem("f_zero")
        f_tmp = sem("f_tmp")
        f_hi = sem("f_hi")
        f_rows = sem("f_rows")
        f_stored = sem("f_stored")
        xt_in = [sem(f"xt_in{k}") for k in range(2)]
        toep_in = [sem(f"toep_in{k}") for k in range(NSUB)]
        proj_done = sem("proj_done")
        proj_used = sem("proj_used")
        nrm_part = sem("nrm_part")
        nrm_ready = sem("nrm_ready")
        norm_done = sem("norm_done")
        ebits_ready = sem("ebits_ready")
        scale_ready = sem("scale_ready")
        yh_ready = sem("yh_ready")
        yl_ready = sem("yl_ready")
        toep_done = sem("toep_done")
        toep_high = sem("toep_high")
        toep_low = sem("toep_low")
        pre_done = sem("pre_done")
        pv_ready = sem("pv_ready")
        pb_hi = sem("pb_hi")
        pb_ready = sem("pb_ready")
        st_done = sem("st_done")
        st_copied = sem("st_copied")
        mult_done = sem("mult_done")
        gz_ready = sem("gz_ready")
        inv_done = sem("inv_done")
        gated = sem("gated")
        y3_out = [sem(f"y3_out{k}") for k in range(4)]

        block = ctx.enter_context(nc.Block())

        @block.sync
        def _(sp):
            for k in range(4):
                sp.sem_inc(y3_out[k], 16)
            sp.dma_start(wf[:], WF).then_inc(s_wf, 16)
            sp.dma_start(posr[:], POSR).then_inc(s_wf, 16)
            sp.dma_start(bfc[:], BFC).then_inc(s_wf, 16)
            sp.wait_ge(f_rows, 6)
            sp.dma_start(fscr_ap.rearrange("(m p) l -> p m l", p=P),
                         frow[:].rearrange("p m l h -> p m (l h)")).then_inc(f_stored, 16)
            for a in range(2):
                sp.dma_start(xt[:, a], XT[:, :, a]).then_inc(xt_in[a], 16)
            sp.dma_start(wi[:, 0].rearrange("p (k h) -> p k h", k=KT), WGT).then_inc(w_in, 16)
            sp.dma_start(wi[:, 1].rearrange("p (k h) -> p k h", k=KT), WUT).then_inc(w_in, 16)
            sp.dma_start(wi[:, 2].rearrange("p (k h) -> p k h", k=HM), WDT).then_inc(w_in, 16)
            sp.wait_ge(f_stored, 16)
            with sp.Fori(0, NG) as g:
                for a in range(2, NA):
                    sp.wait_ge(proj_done, g * NA + a - 1 + 1)
                    sp.dma_start(xt[:, a % 2], XT[:, :, a]).then_inc(xt_in[a % 2], 16)
                with sp.Fori(0, NS) as i:
                    n = g * NS + i
                    for u in range(NSUB):
                        sp.wait_ge(toep_done, n * NSUB + u + 1)
                        src = bass.AP(tensor=fscr_ap.tensor, offset=(i * D + g * CG + u * CS) * (2 * NL),
                                      ap=[[2, P], [2 * NL, CS], [1, 2 * P]])
                        sp.dma_start(toep[:, u], src).then_inc(toep_in[u], 16)
                for a in range(2):
                    sp.wait_ge(proj_done, g * NA + NA + 1)
                    sp.dma_start(xt[:, a], XT[:, :, a]).then_inc(xt_in[a], 16)
                for q in range(4):
                    sp.wait_ge(gated, g * NS * NA + (NS - 1) * NA + 4 * q + 4 + 1)
                    sp.dma_start(y3_ap[bass.ds(g, 1)].rearrange("o p (a w) -> p (o a) w", w=W)[:, 4 * q:4 * q + 4],
                                 xp[:, 4 * q:4 * q + 4, 0]).then_inc(y3_out[q], 16)
            for q in range(4):
                sp.wait_ge(y3_out[q], (NG + 1) * 16)
            for a in range(2):
                sp.wait_ge(xt_in[a], (NG * NA // 2 + 1) * 16)

        @block.tensor
        def _(pe):
            pe.sem_inc(proj_done, 1)
            pe.sem_inc(toep_done, NSUB)
            pe.sem_inc(inv_done, 1)
            pe.wait_ge(s_wf, 48)
            for m in range(6):
                for h in range(2):
                    mm = pe.matmul(bank[m][:, 0:P], wf[:, h, m * P:(m + 1) * P],
                                   posr[:, h, :], start=(h == 0), stop=(h == 1))
                mm.then_inc(f_done, 1)
            pe.wait_ge(s_const, 48)
            pe.wait_ge(f_tmp, 6)
            with pe.Fori(0, NG) as g:
                for a in range(NA):
                    pair = 2 - 2 * (a % 2)
                    pe.wait_ge(proj_used, g * NA + max(a - 1, 0) + 1)
                    if a == 1:
                        pe.wait_ge(gated, g * NS * NA + 1)
                    pe.wait_ge(xt_in[a % 2], g * (NA // 2 * 16) + (a // 2 + 1) * 16)
                    for b in range(NB):
                        for k in range(KT):
                            mm = pe.matmul(bank[pair + b // 2][:, (b % 2) * W:(b % 2 + 1) * W],
                                           xt[:, a % 2, k, b, :], wp[:, k, bass.ds(g, 1), :],
                                           start=(k == 0), stop=(k == KT - 1))
                    mm.then_inc(proj_done, 1)
                with pe.Fori(0, NS) as i:
                    n = g * NS + i
                    pe.wait_ge(nrm_ready, n + 1)
                    pe.matmul(b_pre[:, 0:1], ones[:], nsum[:], start=True, stop=True).then_inc(norm_done, 1)
                    for u in range(NSUB):
                        pe.wait_ge(toep_in[u], n * 16 + 16)
                        if u >= 2:
                            pe.wait_ge(toep_low, n * NSUB + u - 1)
                        for c in range(CS):
                            if c == 0 or (u == 0 and c == CS // 2):
                                piece = u + 2 if u else c // (CS // 2) + 1
                                pe.wait_ge(yh_ready, n * len(PIECES) + piece)
                                pe.wait_ge(yl_ready, n * len(PIECES) + piece)
                            lag = toep[:, u, c, :].rearrange("p (t h) -> p h t", h=2)
                            cols = slice((u * CS + c) * NB, (u * CS + c + 1) * NB)
                            dst = bank[2 * (u % 2) + c // 8][:, (c % 8) * 64:(c % 8 + 1) * 64]
                            pe.matmul(dst, lag[:, 0], yh[:, :, cols], start=True, stop=False)
                            pe.matmul(dst, lag[:, 0], yl[:, :, cols], start=False, stop=False)
                            mm = pe.matmul(dst, lag[:, 1], yh[:, :, cols], start=False, stop=True)
                        mm.then_inc(toep_done, 1)
                    pe.wait_ge(s_tab, 96)
                    for k in range(NA + LAG):
                        if k < NA - 1:
                            pe.wait_ge(st_copied, n * (NA - 1) + k + 1)
                            for q, (e, y) in enumerate(((0, yh), (0, yl), (2, yh))):
                                for h in range(2):
                                    mm = pe.matmul(b_state[:, h * W:(h + 1) * W], ef[:, k, e + h, :], y[:, k, :],
                                                   start=(k == 0 and q == 0 and h == 0),
                                                   stop=(k == NA - 2 and q == 2), skip_group_check=True)
                            mm.then_inc(st_done, 1)
                        if k == 0:
                            for a in range(NA - 1):
                                for y in (yh, yl):
                                    mm = pe.matmul(b_pre[0:P // 2, 0:W], step[:, a, :], y[:, a, :],
                                                   start=(a == 0 and y is yh), stop=(a == NA - 2 and y is yl))
                            mm.then_inc(pre_done, 1)
                        if k >= LAG:
                            a = k - LAG
                            dst = bank[a % 2][:, 0:W]
                            if a <= 1:
                                pe.wait_ge(toep_low, n * NSUB + NSUB)
                            else:
                                pe.wait_ge(gated, n * NA + a - 1 + 1)
                            for h in range(2):
                                mm = pe.matmul(dst, flip[:], dsum[:, a, :, h, :],
                                               start=(h == 0), stop=(h == 1 and a == 0))
                            if a >= 1:
                                if a == 1:
                                    pe.wait_ge(pb_ready, n + 1)
                                pe.matmul(dst, sel[0:P // 2, a, :], pb[0:P // 2, :], start=False, stop=False)
                                pe.wait_ge(gz_ready, n * (NA - 1) + a + 1)
                                for h in range(2):
                                    mm = pe.matmul(dst, ei[:, h, a * P:(a + 1) * P], gz[:, (a - 1) % 3, h, :],
                                                   start=False, stop=(h == 1))
                            mm.then_inc(inv_done, 1)

        @block.scalar
        def _(act):
            act.sem_inc(nrm_part, len(SEG))
            act.sem_inc(st_copied, 1)
            act.dma_start(wp[:], WPG).then_inc(s_const, 16)
            act.dma_start(bp[:], BPG.partition_broadcast(P)).then_inc(s_const, 16)
            act.dma_start(ones[:], ONES).then_inc(s_const, 16)
            act.dma_start(bfr[:], BFR.partition_broadcast(P)).then_inc(s_tab, 16)
            act.dma_start(step[:], STEP).then_inc(s_tab, 16)
            act.dma_start(sel[:], SEL).then_inc(s_tab, 16)
            act.dma_start(flip[:], FLIP).then_inc(s_tab, 16)
            act.dma_start(ef[:], EF).then_inc(s_tab, 16)
            act.dma_start(ei[:], EI).then_inc(s_tab, 16)
            for m in range(6):
                act.wait_ge(f_tmp, m + 1)
                act.wait_ge(f_zero, 1)
                nc.scalar.activation(frow[:, m, 0:P, 0], ftmp[:, m * P:(m + 1) * P], ACT.Copy).then_inc(f_hi, 1)

            act.wait_ge(w_in, 48)
            for wt, q in ((wg, 0), (wu, 1), (wd, 2)):
                nc.scalar.activation(wt[:].rearrange("p k h -> p (k h)"), wi[:, q], ACT.Copy).then_inc(w_cast, 1)

            def square(seg, before):
                act.wait_ge(nrm_part, before + len(SEG))
                first, end = (0,) + SEG, SEG
                nc.scalar.activation(junk[:, 0:end[seg] - first[seg]], xp[:, first[seg]:end[seg], 0, :], ACT.Square,
                                     accum_out=nrm[:, seg:seg + 1]).then_inc(nrm_part, 1)

            with act.Fori(0, NG) as g:
                for seg, end in enumerate(SEG):
                    act.wait_ge(proj_used, g * NA + end + 1)
                    square(seg, g * (len(SEG) * (NS + 1)) + seg)
                with act.Fori(0, NS) as i:
                    n = g * NS + i
                    squares = g * (len(SEG) * (NS + 1)) + i * len(SEG) + len(SEG)
                    act.wait_ge(scale_ready, n + 1)
                    for c0, c1 in PIECES:
                        nc.scalar.activation(yh[:, :, c0:c1], xp[:, :, 0, c0:c1], ACT.Copy,
                                             scale=scale).then_inc(yh_ready, 1)
                    for u in range(NSUB):
                        act.wait_ge(toep_done, n * NSUB + u + 1 + NSUB)
                        for h in range(2):
                            cols = slice(h * SW // 2, (h + 1) * SW // 2)
                            last = nc.scalar.activation(
                                dsum[:, :, u, 0, cols].rearrange("p a (c b) -> p c a b", b=NB),
                                bank[2 * (u % 2) + h][:, :].rearrange("p (c a b) -> p c a b", c=8, b=NB), ACT.Copy)
                        last.then_inc(toep_high, 1)
                    for k in range(NA - 1):
                        act.wait_ge(st_done, n * (NA - 1) + k + 1)
                        act.wait_ge(mult_done, n * (NA - 1) + max(k - 1, 0) + 1)
                        nc.scalar.copy(b_copy[k % 2][:, :], b_state[:, :]).then_inc(st_copied, 1)
                        if k == 1:
                            act.wait_ge(pv_ready, n + 1)
                            nc.scalar.activation(pb[0:P // 2, :], pv[0:P // 2, :], ACT.Copy).then_inc(pb_hi, 1)
                        if k in (7, 11):
                            seg = (k - 7) // 4
                            act.wait_ge(gated, n * NA + SEG[seg] + 1)
                            square(seg, squares + seg)
                    for seg in (2, 3, 4):
                        act.wait_ge(gated, n * NA + SEG[seg] + 1)
                        square(seg, squares + seg)

        @block.vector
        def _(dve):
            dve.sem_inc(gated, 1)
            dve.sem_inc(proj_used, 1)
            dve.sem_inc(mult_done, 1)
            nc.vector.memset(frow[:, :, P:NL, :], 0.0).then_inc(f_zero, 1)
            dve.wait_ge(s_wf, 48)
            for m in range(6):
                dve.wait_ge(f_done, m + 1)
                nc.vector.tensor_scalar(ftmp[:, m * P:(m + 1) * P], bank[m][:, 0:P],
                                        bfc[:, m:m + 1], None, ALU.add).then_inc(f_tmp, 1)
            for m in range(6):
                dve.wait_ge(f_hi, m + 1)
                nc.vector.tensor_tensor(frow[:, m, 0:P, 1], ftmp[:, m * P:(m + 1) * P],
                                        frow[:, m, 0:P, 0], ALU.subtract).then_inc(f_rows, 1)
            dve.wait_ge(s_const, 48)
            with dve.Fori(0, NG) as g:
                for a in range(NA):
                    if a % 4 == 0:
                        dve.wait_ge(y3_out[a // 4], g * 16 + 16)
                        dve.wait_ge(nrm_part, g * (len(SEG) * (NS + 1)) + (a // 4 + 1 if a < 12 else len(SEG)))
                    if a == 10:
                        dve.wait_ge(w_cast, 3)
                    dve.wait_ge(proj_done, g * NA + a + 1 + 1)
                    for h in range(2):
                        last = nc.vector.tensor_tensor(
                            xp[:, a].rearrange("p s (c b) -> p (s c) b", b=NB)[:, :, 2 * h:2 * h + 2],
                            bank[2 - 2 * (a % 2) + h][:, :].rearrange("p (b c) -> p c b", b=2),
                            bp[:, bass.ds(g, 1), :].rearrange("p o c -> p (o c)").unsqueeze(2).broadcast_to(
                                [P, (NS + 1) * CG, 2]), ALU.add)
                    last.then_inc(proj_used, 1)
                with dve.Fori(0, NS) as i:
                    n = g * NS + i
                    dve.wait_ge(nrm_part, g * (len(SEG) * (NS + 1)) + i * len(SEG) + 2 * len(SEG))
                    nc.vector.tensor_reduce(nsum[:], nrm[:], AX_X, ALU.add).then_inc(nrm_ready, 1)
                    dve.wait_ge(norm_done, n + 1)
                    nc.vector.tensor_scalar(ebits[:], b_pre[:, 0:1].bitcast(I32), 24, None,
                                            ALU.logical_shift_right).then_inc(ebits_ready, 1)
                    dve.wait_ge(ebits_ready, n + 1)
                    nc.vector.tensor_scalar(scl[:], ebits[:], -float(1 << 23), float(199 << 23), ALU.mult, ALU.add)
                    nc.vector.tensor_scalar(iscl[:], ebits[:], float(1 << 23), float(55 << 23), ALU.mult,
                                            ALU.add).then_inc(scale_ready, 1)
                    dve.wait_ge(scale_ready, n + 1)
                    for q, (c0, c1) in enumerate(PIECES):
                        dve.wait_ge(yh_ready, n * len(PIECES) + q + 1)
                        nc.vector.scalar_tensor_tensor(
                            out=yl[:, :, c0:c1], in0=xp[:, :, 0, c0:c1], scalar=scale,
                            in1=yh[:, :, c0:c1], op0=ALU.mult, op1=ALU.subtract).then_inc(yl_ready, 1)

                    def spread(t, rep):
                        v = t.unsqueeze(1).unsqueeze(3).broadcast_to([P, rep, CG, NB])
                        return v

                    for u in range(NSUB):
                        dve.wait_ge(toep_high, n * NSUB + u + 1)
                        for h in range(2):
                            cols = slice(h * SW // 2, (h + 1) * SW // 2)
                            last = nc.vector.tensor_tensor(
                                dsum[:, :, u, 1, cols].rearrange("p a (c b) -> p c a b", b=NB),
                                bank[2 * (u % 2) + h][:, :].rearrange("p (c a b) -> p c a b", c=8, b=NB),
                                dsum[:, :, u, 0, cols].rearrange("p a (c b) -> p c a b", b=NB), ALU.subtract)
                        last.then_inc(toep_low, 1)
                    dve.wait_ge(s_tab, 96)
                    for k in range(NA + LAG):
                        if k < NA - 1:
                            dve.wait_ge(st_copied, n * (NA - 1) + k + 1 + 1)
                            dve.wait_ge(gz_ready, n * (NA - 1) + max(k - 1, 0) + 1)
                            for h in range(2):
                                last = nc.vector.tensor_tensor(
                                    prod[:, k % 2, h].rearrange("p (r c b) -> p r c b", r=2, b=NB),
                                    b_copy[k % 2][:, :].rearrange("p (r c b) -> p r c b", r=2, b=NB),
                                    spread(wf[:, h, bass.ds(i * D + g * CG, CG)], 2), ALU.mult)
                            last.then_inc(mult_done, 1)
                        if k == 0:
                            dve.wait_ge(pre_done, n + 1)
                            nc.vector.scalar_tensor_tensor(
                                out=pv[0:P // 2, :].rearrange("p (c b) -> p c b", b=NB),
                                in0=b_pre[0:P // 2, 0:W].rearrange("p (c b) -> p c b", b=NB), scalar=BSC,
                                in1=bfr[0:P // 2, bass.ds(i * D + g * CG, CG)].unsqueeze(2).broadcast_to(
                                    [P // 2, CG, NB]), op0=ALU.mult, op1=ALU.mult).then_inc(pv_ready, 1)
                        if k == 1:
                            dve.wait_ge(pb_hi, n + 1)
                            nc.vector.tensor_tensor(pb[32:64, :], pv[32:64, :], pb[32:64, :],
                                                    ALU.subtract).then_inc(pb_ready, 1)
                        if k >= LAG:
                            a = k - LAG
                            dve.wait_ge(inv_done, n * NA + a + 1 + 1)
                            nc.vector.scalar_tensor_tensor(
                                out=xp[:, a, 0, :], in0=bank[a % 2][:, 0:W], scalar=unscale,
                                in1=xp[:, a, bass.ds(i + 1, 1), :].rearrange("p o w -> p (o w)"),
                                op0=ALU.mult, op1=ALU.mult).then_inc(gated, 1)

        @block.gpsimd
        def _(pool):
            pool.sem_inc(gz_ready, 1)
            with pool.Fori(0, NG) as g:
                with pool.Fori(0, NS) as i:
                    n = g * NS + i
                    for k in range(NA - 1):
                        pool.wait_ge(mult_done, n * (NA - 1) + k + 1 + 1)
                        pool.wait_ge(inv_done, n * NA + max(k - 1, 0) + 1)
                        pa, pbt = prod[:, k % 2, 0], prod[:, k % 2, 1]
                        nc.gpsimd.tensor_tensor(gz[:, k % 3, 0], pa[:, 0:W], pbt[:, W:2 * W], ALU.add)
                        nc.gpsimd.tensor_tensor(gz[:, k % 3, 1], pbt[:, 0:W], pa[:, W:2 * W],
                                                ALU.subtract).then_inc(gz_ready, 1)

    with ExitStack() as ctx:
        def sb(name, shape, dt=F32):
            return ctx.enter_context(nc.sbuf_tensor(name, shape, dt))

        def sem(name):
            return ctx.enter_context(nc.semaphore(name))

        def psum(name):
            return ctx.enter_context(nc.psum_tensor(name, [P, 512], F32))

        ident = sb("ident", [P, P])
        ya = sb("ya", [P, 2, NG, W])
        xr = sb("xr", [P, 2, NB, D])
        x1 = sb("x1", [P, 2, NB, D])
        x1n = sb("x1n", [P, 3, NB, D])
        xh = sb("xh", [P, 2, KT, NTOK], F16)
        xl = sb("xl", [P, 2, KT, NTOK], F16)
        sg = sb("sg", [P, 2, NTOK])
        hf = sb("hf", [P, 2, NTOK])
        hh = sb("hh", [P, 2, HM, NTOK], F16)
        hl = sb("hl", [P, 2, HM, NTOK], F16)
        zz = sb("zz", [P, NB, D])
        oo = sb("oo", [P, 2, NB, D])
        st = sb("st", [P, 2, NB, 6])
        mv = sb("mv", [P, 2, NB, 2])
        rs = sb("rs", [P, 2, NB])
        mhalf = sb("mhalf", [P, NB])
        epst = sb("epst", [P, NB])
        tick = sb("tick", [P, 1])
        b_t = [psum(f"bt{k}") for k in range(KT)]
        b_g = [psum(f"bg{k}") for k in range(2)]
        b_u = [psum(f"bu{k}") for k in range(2)]
        b_d = [psum(f"bd{k}") for k in range(2)]

        id_in = sem("id_in")
        ya_in = [sem(f"ya_in{k}") for k in range(2)]
        xr_in = [sem(f"xr_in{k}") for k in range(2)]
        x1_ready = sem("x1_ready")
        stats = sem("stats")
        mean_ready = sem("mean_ready")
        var_ready = sem("var_ready")
        rstd = sem("rstd")
        const_ready = sem("const_ready")
        x1n_ready = sem("x1n_ready")
        tr_done = sem("tr_done")
        xh_ready = sem("xh_ready")
        xl_ready = sem("xl_ready")
        g_done = sem("g_done")
        u_done = sem("u_done")
        sg_ready = sem("sg_ready")
        hf_ready = sem("hf_ready")
        hh_ready = sem("hh_ready")
        hl_ready = sem("hl_ready")
        d_done = sem("d_done")
        zz_ready = sem("zz_ready")
        oo_ready = sem("oo_ready")
        out_done = [sem(f"out_done{k}") for k in range(2)]

        block = ctx.enter_context(nc.Block())
        xview = X.rearrange("b (a t) d -> t a b d", t=P)
        oview = OUT.rearrange("b (a t) d -> t a b d", t=P)
        yview = y3_ap.rearrange("g p (a w) -> p a g w", w=W)

        @block.sync
        def _(sp):
            for par in range(2):
                sp.sem_inc(out_done[par], 16)

            def load(k, par):
                sp.dma_start(ya[:, par], yview[:, bass.ds(k, 1)].rearrange("p o g w -> p (o g) w")).then_inc(ya_in[par], 16)
                sp.dma_start(xr[:, par], xview[:, bass.ds(k, 1)].rearrange("p o b d -> p (o b) d")).then_inc(xr_in[par], 16)

            load(0, 0)
            load(1, 1)
            sp.dma_start(ident[:], IDENT).then_inc(id_in, 16)
            for k in range(2):
                sp.wait_ge(x1_ready, k + 1)
                load(k + 2, k)

            def store(k, par):
                sp.wait_ge(oo_ready, k * NB + NB + 1)
                sp.dma_start(oview[:, bass.ds(k, 1)].rearrange("p o b d -> p (o b) d"), oo[:, par]).then_inc(out_done[par], 16)

            with sp.Fori(0, NA // 2 - 2) as kk:
                for par in range(2):
                    k = kk * 2 + par
                    sp.wait_ge(x1_ready, k + 3)
                    load(k + 4, par)
                    store(k, par)
            for k in range(NA - 4, NA):
                store(k, k % 2)
            sp.wait_ge(out_done[0], (NA // 2 + 1) * 16)
            sp.wait_ge(out_done[1], (NA // 2 + 1) * 16)

        def rounds(fori, body):
            with fori(0, 2) as q:
                for r in range(1, 7):
                    body(q * 6 + r, r % 2, r % 3, True)
            for k in range(13, NA):
                body(k, k % 2, k % 3, k + 1 < NA)

        @block.tensor
        def _(pe):
            def transposes(k, r3):
                pe.wait_ge(x1n_ready, k * NB + NB)
                pe.wait_ge(xl_ready, k * KT)
                for t in range(KT):
                    for b in range(NB):
                        mm = pe.transpose(b_t[t][:, b * P:(b + 1) * P], x1n[:, r3, b, t * P:(t + 1) * P], ident[:])
                    mm.then_inc(tr_done, 1)

            def gate_up(k, r2, m):
                for wt, bk, free, done in ((wg, b_g, sg_ready, g_done), (wu, b_u, hf_ready, u_done)):
                    pe.wait_ge(free, k * HM + m - 1 if m >= 2 else k * HM)
                    for t in range(KT):
                        for y in (xh, xl):
                            mm = pe.matmul(bk[m % 2][:, :], wt[:, t, m * P:(m + 1) * P], y[:, r2, t, :],
                                           start=(t == 0 and y is xh), stop=(t == KT - 1 and y is xl))
                    mm.then_inc(done, 1)

            def down(k, r2):
                pe.wait_ge(hh_ready, k * HM + HM)
                pe.wait_ge(hl_ready, k * HM + HM)
                for b in range(NB):
                    if b % 2 == 0:
                        pe.wait_ge(zz_ready, k * 2 + b // 2 + 1)
                    for m in range(HM):
                        for h in (hh, hl):
                            mm = pe.matmul(b_d[b // 2][:, (b % 2) * D:(b % 2 + 1) * D],
                                           h[:, r2, m, b * P:(b + 1) * P], wd[:, m, :],
                                           start=(m == 0 and h is hh), stop=(m == HM - 1 and h is hl))
                    if b % 2:
                        mm.then_inc(d_done, 1)

            def step(k, r2, r3, has_next):
                pe.wait_ge(xh_ready, k * KT + KT)
                pe.wait_ge(xl_ready, k * KT + KT)
                for m in range(HM):
                    gate_up(k, r2, m)
                    if m == 1 and not (isinstance(k, int) and k == 0):
                        down(k - 1, 1 - r2)
                    if m == 3 and has_next:
                        transposes(k + 1, (r3 + 1) % 3)

            pe.wait_ge(id_in, 16)
            transposes(0, 0)
            step(0, 0, 0, True)
            rounds(pe.Fori, step)
            down(NA - 1, (NA - 1) % 2)

        @block.scalar
        def _(act):
            def split_x(k, par):
                act.wait_ge(tr_done, k * KT + KT)
                for t in range(KT):
                    nc.scalar.activation(xh[:, par, t, :], b_t[t][:, :], ACT.Copy, scale=XS).then_inc(xh_ready, 1)

            def step(k, r2, r3, has_next):
                for m in range(HM + 1):
                    if m < HM:
                        act.wait_ge(g_done, k * HM + m + 1)
                        act.wait_ge(hf_ready, k * HM + m - 1 if m >= 2 else k * HM)
                        nc.scalar.activation(sg[:, m % 2, :], b_g[m % 2][:, :], ACT.Silu,
                                             scale=QS / XS).then_inc(sg_ready, 1)
                    if m >= 1:
                        act.wait_ge(hf_ready, k * HM + m)
                        nc.scalar.activation(hh[:, r2, m - 1, :], hf[:, (m - 1) % 2, :], ACT.Copy).then_inc(hh_ready, 1)
                    if m == 4 and has_next:
                        split_x(k + 1, 1 - r2)

            split_x(0, 0)
            step(0, 0, 0, True)
            rounds(act.Fori, step)

        @block.vector
        def _(dve):
            def row_stats(src, slot, count):
                for b in range(NB):
                    last = nc.vector.bn_stats(st[:, slot, b, :], src[:, b, :])
                last.then_inc(stats, 1)
                dve.wait_ge(stats, count)
                nc.vector.memset(tick[:], 0.0)
                for b in range(NB):
                    last = nc.vector.bn_aggr(mv[:, slot, b, :], st[:, slot, b, :])
                last.then_inc(mean_ready, 1)

            def normalise(dst, src, slot, count, done):
                dve.wait_ge(rstd, count)
                for b in range(NB):
                    nc.vector.tensor_scalar(dst[:, b, :], src[:, b, :], mv[:, slot, b, 0:1], rs[:, slot, b:b + 1],
                                            ALU.subtract, ALU.mult).then_inc(done, 1)

            def stats1(k, r2, count):
                dve.wait_ge(x1_ready, k + 1)
                row_stats(x1[:, r2], 0, count)

            def norm1(k, r2, r3, count):
                normalise(x1n[:, r3], x1[:, r2], 0, count, x1n_ready)

            def split_x(k, r2):
                for t in range(KT):
                    dve.wait_ge(xh_ready, k * KT + t + 1)
                    nc.vector.scalar_tensor_tensor(out=xl[:, r2, t, :], in0=b_t[t][:, :], scalar=XS,
                                                   in1=xh[:, r2, t, :], op0=ALU.mult,
                                                   op1=ALU.subtract).then_inc(xl_ready, 1)

            def product(k, m):
                dve.wait_ge(u_done, k * HM + m + 1)
                dve.wait_ge(sg_ready, k * HM + m + 1)
                dve.wait_ge(hl_ready, k * HM + m - 1 if m >= 2 else k * HM)
                nc.vector.scalar_tensor_tensor(out=hf[:, m % 2, :], in0=b_u[m % 2][:, :], scalar=HS * QS / XS,
                                               in1=sg[:, m % 2, :], op0=ALU.mult,
                                               op1=ALU.mult).then_inc(hf_ready, 1)

            def sum2(k, r3):
                dve.wait_ge(oo_ready, k * NB + 1)
                for h in range(2):
                    dve.wait_ge(d_done, k * 2 + h + 1)
                    nc.vector.scalar_tensor_tensor(
                        out=zz[:, 2 * h:2 * h + 2, :], in0=b_d[h][:, :].rearrange("p (b c) -> p b c", b=2),
                        scalar=QS / HS, in1=x1n[:, r3, 2 * h:2 * h + 2, :], op0=ALU.mult,
                        op1=ALU.add).then_inc(zz_ready, 1)

            def stats2(k, count):
                dve.wait_ge(zz_ready, k * 2 + 2 + 1)
                row_stats(zz, 1, count)

            def norm2(k, r2, free, count):
                dve.wait_ge(out_done[r2], free)
                normalise(oo[:, r2], zz, 1, count, oo_ready)

            def step(k, r2, r3, has_next):
                start = isinstance(k, int) and k == 0
                c1 = 2 if start else k * 2 + 1
                c2 = k * 2 + 2 if has_next else k * 2 + 1
                free = 0 if start else ((k - 1 - (1 - r2)) * 8 + 16)
                for m in range(HM):
                    product(k, m)
                    if m == 0 and has_next:
                        stats1(k + 1, 1 - r2, c1)
                    if m == 1:
                        if has_next:
                            norm1(k + 1, 1 - r2, (r3 + 1) % 3, c1)
                        if not start:
                            sum2(k - 1, (r3 + 2) % 3)
                    if m == 2 and not start:
                        stats2(k - 1, c2)
                    if m == 3 and has_next:
                        split_x(k + 1, 1 - r2)
                    if m == 4 and not start:
                        norm2(k - 1, 1 - r2, free, c2)

            nc.vector.memset(epst[:], EPS)
            nc.vector.memset(mhalf[:], -0.5).then_inc(const_ready, 1)
            dve.sem_inc(zz_ready, 1)
            dve.sem_inc(oo_ready, 1)
            stats1(0, 0, 1)
            norm1(0, 0, 0, 1)
            split_x(0, 0)
            step(0, 0, 0, True)
            rounds(dve.Fori, step)
            sum2(NA - 1, (NA - 1) % 3)
            stats2(NA - 1, 2 * NA)
            norm2(NA - 1, 1, NA // 2 * 16, 2 * NA)

        @block.gpsimd
        def _(pool):
            def add_x(k, r2):
                pool.wait_ge(ya_in[r2], (k - r2) * 8 + 16)
                pool.wait_ge(xr_in[r2], (k - r2) * 8 + 16)
                nc.gpsimd.tensor_tensor(x1[:, r2].rearrange("p b (g c) -> p b g c", g=NG),
                                        ya[:, r2].rearrange("p g (c b) -> p b g c", b=NB),
                                        xr[:, r2].rearrange("p b (g c) -> p b g c", g=NG), ALU.add).then_inc(x1_ready, 1)

            def root(slot, count):
                pool.wait_ge(mean_ready, count)
                nc.gpsimd.tensor_tensor(rs[:, slot], mv[:, slot, :, 1], epst[:], ALU.add).then_inc(var_ready, 1)
                pool.wait_ge(var_ready, count)
                nc.gpsimd.tensor_tensor(rs[:, slot], rs[:, slot], mhalf[:], ALU.pow).then_inc(rstd, 1)

            def step(k, r2, r3, has_next):
                start = isinstance(k, int) and k == 0
                c1 = 2 if start else k * 2 + 1
                c2 = k * 2 + 2 if has_next else k * 2 + 1
                for m in range(HM):
                    if m == 0 and has_next:
                        root(0, c1)
                    pool.wait_ge(hh_ready, k * HM + m + 1)
                    nc.gpsimd.tensor_tensor(hl[:, r2, m, :], hf[:, m % 2, :], hh[:, r2, m, :],
                                            ALU.subtract).then_inc(hl_ready, 1)
                    if m == 2 and not start:
                        root(1, c2)
                    if m == 3 and not (isinstance(k, int) and k + 2 >= NA):
                        pool.wait_ge(x1n_ready, k * NB + NB)
                        add_x(k + 2, r2)

            pool.wait_ge(const_ready, 1)
            add_x(0, 0)
            add_x(1, 1)
            root(0, 1)
            step(0, 0, 0, True)
            rounds(pool.Fori, step)
            root(1, 2 * NA)

    whole.close()


def tables():
    k = np.arange(P)
    period = np.power(np.float32(10000.0), (2 * k).astype(np.float32) / np.float32(D)).astype(np.float32)
    t = np.arange(T)
    lag_angle = (t[:P, None].astype(np.float32) / period[None, :]).astype(np.float32).astype(np.float64)
    angle = t[:, None].astype(np.float64) / period[None, :].astype(np.float64)
    sin, cos = np.sin(angle), np.cos(angle)
    posr = np.stack([np.sin(lag_angle).T, np.cos(lag_angle).T], 1).astype(np.float32)
    high = [x.astype(np.float16) for x in (cos, sin)]
    low = [(x - h.astype(np.float64)).astype(np.float16) for x, h in zip((cos, sin), high)]
    ef = np.stack(high + low, 0).reshape(4, NA, P, P)[:, :NA - 1].transpose(2, 1, 0, 3)
    ei = np.stack([sin.T, cos.T], 1).astype(np.float32)
    row = np.arange(P)
    step = np.zeros((P, NA - 1, P // 2), np.float16)
    sel = np.zeros((P, NA, P), np.float16)
    for a in range(NA):
        if a < NA - 1:
            step[:, a, (row[:P // 2] % 32 < NA) & (row[:P // 2] % 32 > a)] = 1
        sel[[a, 32 + a], a, :] = 1 / BSC
    flip = (np.eye(P)[::-1]).astype(np.float16)
    return posr[:, :, ::-1], np.ascontiguousarray(ef), ei, step, sel, flip


def kernel(L0_attn_X, L0_attn_Wp, L0_attn_bp, L0_attn_Wf, L0_attn_bf, L0_ffn_w_gate, L0_ffn_w_up, L0_ffn_w_down):
    import concourse.bacc as bacc
    from concourse.bass_utils import run_bass_kernel_spmd

    X = np.asarray(L0_attn_X)
    posr, ef, ei, step, sel, flip = tables()

    def by_group(w):
        return w.reshape(w.shape[:-1] + (NS + 1, NG, CG)).swapaxes(-3, -2).reshape(w.shape[:-1] + (NG, (NS + 1) * CG))

    wf = np.asarray(L0_attn_Wf)
    bf = np.asarray(L0_attn_bf)
    arrays = {
        "XT": X.reshape(NB, NA, P, KT, P).transpose(4, 3, 1, 0, 2),
        "X": X,
        "WPG": by_group(np.asarray(L0_attn_Wp)).reshape(KT, P, NG, (NS + 1) * CG).transpose(1, 0, 2, 3),
        "BPG": by_group(np.asarray(L0_attn_bp)),
        "WF": np.stack([wf[0::2], wf[1::2]], 1),
        "BFC": bf.reshape(NS * D // P, P).T,
        "BFR": bf,
        "POSR": posr, "EF": ef, "EI": ei, "STEP": step, "SEL": sel, "FLIP": flip,
        "ONES": np.ones((P, P), np.float32), "IDENT": np.eye(P, dtype=np.float32),
        "WGT": np.asarray(L0_ffn_w_gate).T.reshape(KT, P, HID).transpose(1, 0, 2),
        "WUT": np.asarray(L0_ffn_w_up).T.reshape(KT, P, HID).transpose(1, 0, 2),
        "WDT": np.asarray(L0_ffn_w_down).T.reshape(HM, P, D).transpose(1, 0, 2),
    }
    nc = bacc.Bacc("TRN2", target_bir_lowering=False, num_devices=1)
    ins, args = {}, []
    for name, a in arrays.items():
        ins[f"in_{name}"] = np.ascontiguousarray(a)
        args.append(nc.dram_tensor(f"in_{name}", a.shape, mybir.dt.from_np(a.dtype), kind="ExternalInput").ap())
    args.append(nc.dram_tensor("out_x", [NB, T, D], F32, kind="ExternalOutput").ap())
    program(nc, *args)
    r = run_bass_kernel_spmd(nc, [ins], core_ids=[0])
    return r.results[0]["out_x"]
```

```python
from contextlib import ExitStack

import numpy as np

import concourse.bass as bass
from concourse import mybir

F32 = mybir.dt.float32
F16 = mybir.dt.float16
I32 = mybir.dt.int32
F32R = mybir.dt.float32r
ALU = mybir.AluOpType
ACT = mybir.ActivationFunctionType

P = 128
SEG = (4, 8, 12, 15, 16)
EARLY = 2
XTS = 3
LAG = 2
NB, T, D = 4, 2048, 256
NS = 3
NA = T // P
SQ = len(SEG) * NS + EARLY
NG, CG = 4, 64
NSUB, CS = 4, 16
W = NB * CG
SW = NB * CS
PIECES = ((0, SW // 4), (SW // 4, SW // 2), (SW // 2, SW)) + tuple((u * SW, (u + 1) * SW) for u in range(1, NSUB))
KT = D // P
NL = 2 * P
HID = 768
HM = HID // P
NTOK = NB * P
EPS = 1e-5
BSC = 2.0 ** -3
XS = 2.0 ** 10
HS = 2.0 ** -2
QS = 1.0 / 127.0


def program(nc, XT, X, WPG, BPG, WF, BFC, BFR, POSR, EF, EI, STEP, SEL, FLIP, ONES, IDENT, WGT, WUT, WDT, OUT):
    fscr = nc.dram_tensor("filter_rows", [NS * D, NL * 2], F16)
    y3scr = nc.dram_tensor("attn_out", [NG, P, NA * W], F32)
    fscr_ap, y3_ap = fscr.ap(), y3scr.ap()

    with ExitStack() as ctx:
        def sb(name, shape, dt=F32):
            return ctx.enter_context(nc.sbuf_tensor(name, shape, dt))

        def sem(name):
            return ctx.enter_context(nc.semaphore(name))

        def psum(name):
            return ctx.enter_context(nc.psum_tensor(name, [P, 512], F32))

        xp = sb("xp", [P, NA, NS + 1, W])
        yh = sb("yh", [P, NA, W], F16)
        yl = sb("yl", [P, NA, W], F16)
        toep = sb("toep", [P, NSUB, CS, 2 * P], F16)
        ef = sb("ef", [P, NA - 1, 4, P], F16)
        ei = sb("ei", [P, 2, T])
        step = sb("step", [P, NA - 1, P // 2], F16)
        sel = sb("sel", [P // 2, NA, P], F16)
        flip = sb("flip", [P, P], F16)
        wf = sb("wf", [P, 2, NS * D])
        wp = sb("wp", [P, KT, (NS + 1) * CG])
        wps = sb("wps", [P, 2, KT, (NS + 1) * CG], F32R)
        bp = sb("bp", [P, NG, (NS + 1) * CG])
        bfr = sb("bfr", [P // 2, NS * D])
        bfc = sb("bfc", [P, NS * D // P])
        xt = sb("xt", [P, XTS, KT, NB, P])
        prod = sb("prod", [P, 2, 2, 2 * W])
        gz = sb("gz", [P, 3, 2, W])
        pv = sb("pv", [P, W])
        pb = sb("pb", [P, W], F16)
        xs = sb("xs", [P, NB, 2, KT, P], F32R)
        nrm = sb("nrm", [P, len(SEG)])
        ebits = sb("ebits", [P, 1], I32)
        scl = sb("scl", [P, 1], I32)
        iscl = sb("iscl", [P, 1], I32)
        ones = sb("ones", [P, P])
        spare = toep[:].rearrange("p u c l -> p (u c l)")
        posr = spare[:, 0:4 * P].bitcast(F32).rearrange("p (h l) -> p h l", h=2)
        ftmp = spare[:, 4 * P:4 * P + 2 * NS * D].bitcast(F32)
        frow = spare[:, 4 * P + 2 * NS * D:4 * P + 2 * NS * D + 6 * 2 * NL].rearrange("p (m l h) -> p m l h", m=6, h=2)

        bank = [psum(f"bank{i}") for i in range(8)]
        b_state, b_copy, b_pre = bank[4], bank[5:7], bank[7]
        junk = yh[:, 0:4]
        scaled = prod[:].rearrange("p r h w -> p (r h w)")[:, 0:NA * SW].rearrange("p (a w) -> p a w", a=NA)
        b_toep = (bank[4:6], bank[6:8], bank[0:2], bank[2:4])
        dsum = xp[:, :, 0, :].bitcast(F16).rearrange("p a (u h w) -> p a u h w", u=NSUB, h=2)
        scale = scl[:, 0:1].bitcast(F32)
        unscale = iscl[:, 0:1].bitcast(F32)

        s_const = sem("s_const")
        s_wf = sem("s_wf")
        s_tab = sem("s_tab")
        f_done = sem("f_done")
        f_zero = sem("f_zero")
        f_tmp = sem("f_tmp")
        f_hi = sem("f_hi")
        f_rows = sem("f_rows")
        f_stored = sem("f_stored")
        xt_in = [sem(f"xt_in{k}") for k in range(XTS)]
        wp_in = sem("wp_in")
        toep_in = [sem(f"toep_in{k}") for k in range(NSUB)]
        wp_hi = sem("wp_hi")
        wp_lo = sem("wp_lo")
        x_hi = sem("x_hi")
        x_lo = sem("x_lo")
        x_lo_dve = sem("x_lo_dve")
        x_used = sem("x_used")
        proj_done = sem("proj_done")
        proj_used = sem("proj_used")
        nrm_part = sem("nrm_part")
        norm_done = sem("norm_done")
        ebits_ready = sem("ebits_ready")
        scale_ready = sem("scale_ready")
        yh_ready = sem("yh_ready")
        yl_ready = sem("yl_ready")
        y_scaled = sem("y_scaled")
        yl_last = sem("yl_last")
        toep_done = sem("toep_done")
        toep_high = sem("toep_high")
        toep_low = sem("toep_low")
        pre_done = sem("pre_done")
        pv_ready = sem("pv_ready")
        pb_hi = sem("pb_hi")
        pb_ready = sem("pb_ready")
        st_done = sem("st_done")
        st_copied = sem("st_copied")
        mult_done = sem("mult_done")
        gz_ready = sem("gz_ready")
        inv_done = sem("inv_done")
        gated = sem("gated")
        y3_out = [sem(f"y3_out{k}") for k in range(4)]

        def arrived(g, a):
            loads = len(range(a % XTS, NA, XTS))
            return g * (loads * 16) + (a // XTS + 1) * 16

        block = ctx.enter_context(nc.Block())

        @block.sync
        def _(sp):
            for k in range(4):
                sp.sem_inc(y3_out[k], 16)
            sp.dma_start(wf[:], WF).then_inc(s_wf, 16)
            sp.dma_start(posr[:], POSR).then_inc(s_wf, 16)
            sp.dma_start(bfc[:], BFC).then_inc(s_wf, 16)
            for a in range(XTS):
                sp.dma_start(xt[:, a], XT[:, :, a]).then_inc(xt_in[a], 16)
            sp.wait_ge(f_rows, 6)
            sp.dma_start(fscr_ap.rearrange("(m p) l -> p m l", p=P),
                         frow[:].rearrange("p m l h -> p m (l h)")).then_inc(f_stored, 16)
            with sp.Fori(0, NG) as g:
                for a in range(XTS, NA):
                    sp.wait_ge(x_lo, (g * NA + a - XTS + 1) * (NB - 1))
                    sp.wait_ge(x_lo_dve, g * NA + a - XTS + 1)
                    sp.dma_start(xt[:, a % XTS], XT[:, :, a]).then_inc(xt_in[a % XTS], 16)
                sp.wait_ge(wp_lo, g + 1)
                sp.dma_start(wp[:], WPG[bass.ds(g + 1, 1)].rearrange("o p k c -> p (o k) c")).then_inc(wp_in, 16)
                sp.wait_ge(f_stored, 16)
                with sp.Fori(0, NS) as i:
                    n = g * NS + i
                    for u in range(NSUB):
                        sp.wait_ge(toep_done, n * NSUB + u + 1)
                        src = bass.AP(tensor=fscr_ap.tensor, offset=(i * D + g * CG + u * CS) * (2 * NL),
                                      ap=[[2, P], [2 * NL, CS], [1, 2 * P]])
                        sp.dma_start(toep[:, u], src).then_inc(toep_in[u], 16)
                for a in range(XTS):
                    sp.wait_ge(x_lo, (g * NA + NA) * (NB - 1))
                    sp.wait_ge(x_lo_dve, g * NA + NA)
                    sp.dma_start(xt[:, a], XT[:, :, a]).then_inc(xt_in[a], 16)
                for q in range(4):
                    sp.wait_ge(gated, g * NS * NA + NS * NA + 4 * q + 4 + 1)
                    sp.dma_start(y3_ap[bass.ds(g, 1)].rearrange("o p (a w) -> p (o a) w", w=W)[:, 4 * q:4 * q + 4],
                                 xp[:, 4 * q:4 * q + 4, 0]).then_inc(y3_out[q], 16)
            for q in range(4):
                sp.wait_ge(y3_out[q], (NG + 1) * 16)
            for a in range(XTS):
                sp.wait_ge(xt_in[a], arrived(NG, a))
            sp.wait_ge(wp_in, (NG + 1) * 16)

        @block.tensor
        def _(pe):
            pe.sem_inc(proj_done, 1)
            pe.sem_inc(toep_done, NSUB)
            pe.sem_inc(inv_done, 1)
            pe.wait_ge(s_wf, 48)
            for m in range(6):
                for h in range(2):
                    mm = pe.matmul(bank[m][:, 0:P], wf[:, h, m * P:(m + 1) * P],
                                   posr[:, h, :], start=(h == 0), stop=(h == 1))
                mm.then_inc(f_done, 1)
            pe.wait_ge(s_const, 32)
            pe.wait_ge(f_tmp, 6)
            with pe.Fori(0, NG) as g:
                pe.wait_ge(wp_lo, g + 1)
                for a in range(NA):
                    pair = 2 - 2 * (a % 2)
                    pe.wait_ge(proj_used, g * NA + max(a - 1, 0) + 1)
                    if a == 1:
                        pe.wait_ge(gated, g * NS * NA + NA + 1)
                    for b in range(NB):
                        if b < NB - 1:
                            pe.wait_ge(x_lo, (g * NA + a) * (NB - 1) + b + 1)
                        else:
                            pe.wait_ge(x_lo_dve, g * NA + a + 1)
                        for k in range(KT):
                            for q, (hx, hw) in enumerate(((0, 0), (0, 1), (1, 0))):
                                mm = pe.matmul(bank[pair + b // 2][:, (b % 2) * W:(b % 2 + 1) * W],
                                               xs[:, b, hx, k, :], wps[:, hw, k, :],
                                               start=(k == 0 and q == 0), stop=(k == KT - 1 and q == 2))
                        if b < NB - 1:
                            mm.then_inc(x_used, 1)
                    mm.then_inc(proj_done, 1)
                with pe.Fori(0, NS) as i:
                    n = g * NS + i
                    for seg in range(len(SEG)):
                        if seg >= EARLY - 1:
                            pe.wait_ge(nrm_part, g * SQ + i * len(SEG) + seg + 1 + len(SEG))
                        mm = pe.matmul(b_pre[:, 0:1], ones[:], nrm[:, seg:seg + 1], start=(seg == 0),
                                       stop=(seg == len(SEG) - 1))
                    mm.then_inc(norm_done, 1)
                    for u in range(NSUB):
                        pe.wait_ge(toep_in[u], n * 16 + 16)
                        for c in range(CS):
                            if u * SW + c * NB in [c0 for c0, _ in PIECES]:
                                piece = [c0 for c0, _ in PIECES].index(u * SW + c * NB) + 1
                                pe.wait_ge(yh_ready, n * len(PIECES) + piece)
                                if piece < len(PIECES):
                                    pe.wait_ge(yl_ready, n * (len(PIECES) - 1) + piece)
                                else:
                                    pe.wait_ge(yl_last, n + 1)
                            lag = toep[:, u, c, :].rearrange("p (t h) -> p h t", h=2)
                            cols = slice((u * CS + c) * NB, (u * CS + c + 1) * NB)
                            dst = b_toep[u][c // 8][:, (c % 8) * 64:(c % 8 + 1) * 64]
                            pe.matmul(dst, lag[:, 0], yh[:, :, cols], start=True, stop=False)
                            pe.matmul(dst, lag[:, 0], yl[:, :, cols], start=False, stop=False)
                            mm = pe.matmul(dst, lag[:, 1], yh[:, :, cols], start=False, stop=True)
                        mm.then_inc(toep_done, 1)
                    pe.wait_ge(s_tab, 96)
                    for k in range(NA + LAG):
                        if k < NA - 1:
                            if k == 0:
                                pe.wait_ge(toep_low, n * NSUB + 1)
                            pe.wait_ge(st_copied, n * (NA - 1) + k + 1)
                            for q, (e, y) in enumerate(((0, yh), (0, yl), (2, yh))):
                                for h in range(2):
                                    mm = pe.matmul(b_state[:, h * W:(h + 1) * W], ef[:, k, e + h, :], y[:, k, :],
                                                   start=(k == 0 and q == 0 and h == 0),
                                                   stop=(k == NA - 2 and q == 2), skip_group_check=True)
                            mm.then_inc(st_done, 1)
                        if k in (0, 1):
                            if k == 0:
                                pe.wait_ge(toep_low, n * NSUB + 2)
                            for a in (range(NA // 2), range(NA // 2, NA - 1))[k]:
                                for y in (yh, yl):
                                    mm = pe.matmul(b_pre[0:P // 2, 0:W], step[:, a, :], y[:, a, :],
                                                   start=(a == 0 and y is yh), stop=(a == NA - 2 and y is yl))
                            if k == 1:
                                mm.then_inc(pre_done, 1)
                        if k >= LAG:
                            a = k - LAG
                            dst = bank[a % 2][:, 0:W]
                            if a <= 1:
                                pe.wait_ge(toep_low, n * NSUB + NSUB)
                            else:
                                pe.wait_ge(gated, n * NA + NA + a - 1 + 1)
                            for h in range(2):
                                mm = pe.matmul(dst, flip[:], dsum[:, a, :, h, :],
                                               start=(h == 0), stop=(h == 1 and a == 0))
                            if a >= 1:
                                if a == 1:
                                    pe.wait_ge(pb_ready, n + 1)
                                pe.matmul(dst, sel[:, a, :], pb[0:P // 2, :], start=False, stop=False)
                                pe.wait_ge(gz_ready, n * (NA - 1) + a + 1)
                                for h in range(2):
                                    mm = pe.matmul(dst, ei[:, h, a * P:(a + 1) * P], gz[:, (a - 1) % 3, h, :],
                                                   start=False, stop=(h == 1))
                            mm.then_inc(inv_done, 1)

        @block.scalar
        def _(act):
            act.sem_inc(nrm_part, len(SEG))
            act.sem_inc(st_copied, 1)
            act.dma_start(wp[:], WPG[0]).then_inc(wp_in, 16)
            act.dma_start(bp[:], BPG.partition_broadcast(P)).then_inc(s_const, 16)
            act.dma_start(ones[:], ONES).then_inc(s_const, 16)
            act.dma_start(bfr[:], BFR.partition_broadcast(P // 2)).then_inc(s_tab, 16)
            act.dma_start(step[:], STEP).then_inc(s_tab, 16)
            act.dma_start(sel[:], SEL).then_inc(s_tab, 16)
            act.dma_start(flip[:], FLIP).then_inc(s_tab, 16)
            for m in range(6):
                act.wait_ge(f_tmp, m + 1)
                act.wait_ge(f_zero, 1)
                nc.scalar.activation(frow[:, m, 0:P, 0], ftmp[:, m * P:(m + 1) * P], ACT.Copy).then_inc(f_hi, 1)
            act.dma_start(ef[:], EF).then_inc(s_tab, 16)
            act.dma_start(ei[:], EI).then_inc(s_tab, 16)

            def square(seg, before):
                act.wait_ge(nrm_part, before + len(SEG))
                first, end = (0,) + SEG, SEG
                nc.scalar.activation(junk[:, 0:end[seg] - first[seg]], xp[:, first[seg]:end[seg], 0, :], ACT.Square,
                                     accum_out=nrm[:, seg:seg + 1]).then_inc(nrm_part, 1)

            with act.Fori(0, NG) as g:
                act.wait_ge(proj_done, g * NA + 1)
                act.wait_ge(wp_in, g * 16 + 16)
                nc.scalar.activation(wps[:, 0], wp[:], ACT.Copy).then_inc(wp_hi, 1)
                for a in range(NA):
                    act.wait_ge(xt_in[a % XTS], arrived(g, a))
                    for b in range(NB):
                        if a >= 1:
                            if b < NB - 1:
                                act.wait_ge(x_used, (g * NA + a - 1) * (NB - 1) + b + 1)
                            else:
                                act.wait_ge(proj_done, g * NA + a + 1)
                        nc.scalar.activation(xs[:, b, 0], xt[:, a % XTS, :, b, :], ACT.Copy).then_inc(x_hi, 1)
                    if a in (6, 10):
                        seg = (a - 6) // 4
                        act.wait_ge(proj_used, g * NA + SEG[seg] + 1)
                        square(seg, g * SQ + seg)
                with act.Fori(0, NS) as i:
                    n = g * NS + i
                    squares = g * SQ + i * len(SEG) + EARLY
                    for seg in range(EARLY, len(SEG)):
                        act.wait_ge(proj_used, g * NA + SEG[seg] + 1)
                        act.wait_ge(gated, n * NA + SEG[seg] + 1)
                        square(seg, squares + seg - EARLY)
                    act.wait_ge(scale_ready, n + 1)
                    for c0, c1 in PIECES:
                        nc.scalar.activation(yh[:, :, c0:c1], xp[:, :, 0, c0:c1], ACT.Copy,
                                             scale=scale).then_inc(yh_ready, 1)
                    for u in range(NSUB):
                        act.wait_ge(toep_done, n * NSUB + u + 1 + NSUB)
                        for h in range(2):
                            cols = slice(h * SW // 2, (h + 1) * SW // 2)
                            last = nc.scalar.activation(
                                dsum[:, :, u, 0, cols].rearrange("p a (c b) -> p c a b", b=NB),
                                b_toep[u][h][:, :].rearrange("p (c a b) -> p c a b", c=8, b=NB), ACT.Copy)
                        last.then_inc(toep_high, 1)
                    for k in range(NA - 1):
                        act.wait_ge(st_done, n * (NA - 1) + k + 1)
                        act.wait_ge(mult_done, n * (NA - 1) + max(k - 1, 0) + 1)
                        nc.scalar.copy(b_copy[k % 2][:, :], b_state[:, :]).then_inc(st_copied, 1)
                        if k == 2:
                            act.wait_ge(pv_ready, n + 1)
                            nc.scalar.activation(pb[0:P // 2, :], pv[0:P // 2, :], ACT.Copy).then_inc(pb_hi, 1)
                        if k in (7, 11):
                            seg = (k - 7) // 4
                            act.wait_ge(gated, n * NA + NA + SEG[seg] + 1)
                            square(seg, squares + len(SEG) - EARLY + seg)

        @block.vector
        def _(dve):
            dve.sem_inc(gated, NA + 1)
            dve.sem_inc(proj_used, 1)
            dve.sem_inc(mult_done, 1)
            nc.vector.memset(frow[:, :, P:NL, :], 0.0).then_inc(f_zero, 1)
            dve.wait_ge(s_wf, 48)
            for m in range(6):
                dve.wait_ge(f_done, m + 1)
                nc.vector.tensor_scalar(ftmp[:, m * P:(m + 1) * P], bank[m][:, 0:P],
                                        bfc[:, m:m + 1], None, ALU.add).then_inc(f_tmp, 1)
            for m in range(6):
                dve.wait_ge(f_hi, m + 1)
                nc.vector.tensor_tensor(frow[:, m, 0:P, 1], ftmp[:, m * P:(m + 1) * P],
                                        frow[:, m, 0:P, 0], ALU.subtract).then_inc(f_rows, 1)
            dve.wait_ge(s_const, 32)
            with dve.Fori(0, NG) as g:
                for a in range(NA):
                    dve.wait_ge(x_hi, (g * NA + a) * NB + NB)
                    nc.vector.tensor_tensor(xs[:, NB - 1, 1], xt[:, a % XTS, :, NB - 1, :],
                                            xs[:, NB - 1, 0].bitcast(F32), ALU.subtract).then_inc(x_lo_dve, 1)
                    if a % 4 == 0:
                        dve.wait_ge(y3_out[a // 4], g * 16 + 16)
                        dve.wait_ge(nrm_part, g * SQ + len(SEG))
                    dve.wait_ge(proj_done, g * NA + a + 1 + 1)
                    for h in range(2):
                        last = nc.vector.tensor_tensor(
                            xp[:, a].rearrange("p s (c b) -> p (s c) b", b=NB)[:, :, 2 * h:2 * h + 2],
                            bank[2 - 2 * (a % 2) + h][:, :].rearrange("p (b c) -> p c b", b=2),
                            bp[:, bass.ds(g, 1), :].rearrange("p o c -> p (o c)").unsqueeze(2).broadcast_to(
                                [P, (NS + 1) * CG, 2]), ALU.add)
                    last.then_inc(proj_used, 1)
                with dve.Fori(0, NS) as i:
                    n = g * NS + i
                    dve.wait_ge(norm_done, n + 1)
                    nc.vector.tensor_scalar(ebits[:], b_pre[:, 0:1].bitcast(I32), 24, None,
                                            ALU.logical_shift_right).then_inc(ebits_ready, 1)
                    dve.wait_ge(ebits_ready, n + 1)
                    nc.vector.tensor_scalar(scl[:], ebits[:], -float(1 << 23), float(199 << 23), ALU.mult, ALU.add)
                    nc.vector.tensor_scalar(iscl[:], ebits[:], float(1 << 23), float(55 << 23), ALU.mult,
                                            ALU.add).then_inc(scale_ready, 1)
                    dve.wait_ge(scale_ready, n + 1)
                    for q, (c0, c1) in enumerate(PIECES[:-1]):
                        dve.wait_ge(yh_ready, n * len(PIECES) + q + 1)
                        nc.vector.scalar_tensor_tensor(
                            out=yl[:, :, c0:c1], in0=xp[:, :, 0, c0:c1], scalar=scale,
                            in1=yh[:, :, c0:c1], op0=ALU.mult, op1=ALU.subtract).then_inc(yl_ready, 1)

                    def spread(t, rep):
                        return t.unsqueeze(1).unsqueeze(3).broadcast_to([P, rep, CG, NB])

                    for u in range(NSUB):
                        dve.wait_ge(toep_high, n * NSUB + u + 1)
                        for h in range(2):
                            cols = slice(h * SW // 2, (h + 1) * SW // 2)
                            last = nc.vector.tensor_tensor(
                                dsum[:, :, u, 1, cols].rearrange("p a (c b) -> p c a b", b=NB),
                                b_toep[u][h][:, :].rearrange("p (c a b) -> p c a b", c=8, b=NB),
                                dsum[:, :, u, 0, cols].rearrange("p a (c b) -> p c a b", b=NB), ALU.subtract)
                        last.then_inc(toep_low, 1)
                    dve.wait_ge(s_tab, 96)
                    dve.wait_ge(yl_last, n + 1)
                    for k in range(NA + LAG):
                        if k == 2:
                            dve.wait_ge(pb_hi, n + 1)
                            nc.vector.tensor_tensor(pb[32:64, :], pv[32:64, :], pb[32:64, :],
                                                    ALU.subtract).then_inc(pb_ready, 1)
                        if k < NA - 1:
                            dve.wait_ge(st_copied, n * (NA - 1) + k + 1 + 1)
                            dve.wait_ge(gz_ready, n * (NA - 1) + max(k - 1, 0) + 1)
                            for h in range(2):
                                last = nc.vector.tensor_tensor(
                                    prod[:, k % 2, h].rearrange("p (r c b) -> p r c b", r=2, b=NB),
                                    b_copy[k % 2][:, :].rearrange("p (r c b) -> p r c b", r=2, b=NB),
                                    spread(wf[:, h, bass.ds(i * D + g * CG, CG)], 2), ALU.mult)
                            last.then_inc(mult_done, 1)
                        if k == 1:
                            dve.wait_ge(pre_done, n + 1)
                            nc.vector.scalar_tensor_tensor(
                                out=pv[0:P // 2, :].rearrange("p (c b) -> p c b", b=NB),
                                in0=b_pre[0:P // 2, 0:W].rearrange("p (c b) -> p c b", b=NB), scalar=BSC,
                                in1=bfr[:, bass.ds(i * D + g * CG, CG)].unsqueeze(2).broadcast_to(
                                    [P // 2, CG, NB]), op0=ALU.mult, op1=ALU.mult).then_inc(pv_ready, 1)
                        if k >= LAG:
                            a = k - LAG
                            dve.wait_ge(inv_done, n * NA + a + 1 + 1)
                            nc.vector.scalar_tensor_tensor(
                                out=xp[:, a, 0, :], in0=bank[a % 2][:, 0:W], scalar=unscale,
                                in1=xp[:, a, bass.ds(i + 1, 1), :].rearrange("p o w -> p (o w)"),
                                op0=ALU.mult, op1=ALU.mult).then_inc(gated, 1)

        @block.gpsimd
        def _(pool):
            pool.sem_inc(gz_ready, 1)
            with pool.Fori(0, NG) as g:
                pool.wait_ge(wp_hi, g + 1)
                nc.gpsimd.tensor_tensor(wps[:, 1], wp[:], wps[:, 0].bitcast(F32), ALU.subtract).then_inc(wp_lo, 1)
                for a in range(NA):
                    for b in range(NB - 1):
                        pool.wait_ge(x_hi, (g * NA + a) * NB + b + 1)
                        nc.gpsimd.tensor_tensor(xs[:, b, 1], xt[:, a % XTS, :, b, :], xs[:, b, 0].bitcast(F32),
                                                ALU.subtract).then_inc(x_lo, 1)
                with pool.Fori(0, NS) as i:
                    n = g * NS + i
                    c0, c1 = PIECES[-1]
                    pool.wait_ge(scale_ready, n + 1)
                    nc.gpsimd.tensor_tensor(scaled[:], xp[:, :, 0, c0:c1], scale.unsqueeze(2).broadcast_to(
                        [P, NA, SW]), ALU.mult).then_inc(y_scaled, 1)
                    pool.wait_ge(y_scaled, n + 1)
                    pool.wait_ge(yh_ready, n * len(PIECES) + len(PIECES))
                    nc.gpsimd.tensor_tensor(yl[:, :, c0:c1], scaled[:], yh[:, :, c0:c1],
                                            ALU.subtract).then_inc(yl_last, 1)
                    for k in range(NA - 1):
                        pool.wait_ge(mult_done, n * (NA - 1) + k + 1 + 1)
                        pool.wait_ge(inv_done, n * NA + max(k - 1, 0) + 1)
                        pa, pbt = prod[:, k % 2, 0], prod[:, k % 2, 1]
                        nc.gpsimd.tensor_tensor(gz[:, k % 3, 0], pa[:, 0:W], pbt[:, W:2 * W], ALU.add)
                        nc.gpsimd.tensor_tensor(gz[:, k % 3, 1], pbt[:, 0:W], pa[:, W:2 * W],
                                                ALU.subtract).then_inc(gz_ready, 1)

    with ExitStack() as ctx:
        def sb(name, shape, dt=F32):
            return ctx.enter_context(nc.sbuf_tensor(name, shape, dt))

        def sem(name):
            return ctx.enter_context(nc.semaphore(name))

        def psum(name):
            return ctx.enter_context(nc.psum_tensor(name, [P, 512], F32))

        ident = sb("ident", [P, P])
        wi = sb("wi", [P, 3, 2 * HID], I32)
        wq = sb("wq", [P, 3, 2 * HID], F16)
        wg = wq[:, 0].rearrange("p (k h) -> p k h", k=KT)
        wu = wq[:, 1].rearrange("p (k h) -> p k h", k=KT)
        wd = wq[:, 2].rearrange("p (k h) -> p k h", k=HM)
        ya = sb("ya", [P, 2, NG, W])
        xr = sb("xr", [P, 2, NB, D])
        x1 = sb("x1", [P, 2, NB, D])
        x1n = sb("x1n", [P, 3, NB, D])
        xh = sb("xh", [P, 2, KT, NTOK], F16)
        xl = sb("xl", [P, 2, KT, NTOK], F16)
        sg = sb("sg", [P, 3, NTOK])
        hf = sb("hf", [P, 3, NTOK])
        hh = sb("hh", [P, 2, HM, NTOK], F16)
        hl = sb("hl", [P, 2, HM, NTOK], F16)
        zz = sb("zz", [P, NB, D])
        oo = sb("oo", [P, 2, NB, D])
        st = sb("st", [P, 2, NB, 6])
        mv = sb("mv", [P, 2, NB, 2])
        rs = sb("rs", [P, 2, NB])
        mhalf = sb("mhalf", [P, NB])
        epst = sb("epst", [P, NB])
        tick = sb("tick", [P, 1])
        b_t = [psum(f"bt{k}") for k in range(KT)]
        b_g = [psum(f"bg{k}") for k in range(2)]
        b_u = [psum(f"bu{k}") for k in range(2)]
        b_d = [psum(f"bd{k}") for k in range(2)]

        id_in = sem("id_in")
        w_in = [sem(f"w_in{q}") for q in range(3)]
        w_cast = sem("w_cast")
        ya_in = [sem(f"ya_in{k}") for k in range(2)]
        xr_in = [sem(f"xr_in{k}") for k in range(2)]
        x1_ready = sem("x1_ready")
        stats = sem("stats")
        mean_ready = sem("mean_ready")
        var_ready = sem("var_ready")
        rstd = sem("rstd")
        const_ready = sem("const_ready")
        x1n_ready = sem("x1n_ready")
        tr_done = sem("tr_done")
        xh_ready = sem("xh_ready")
        xl_ready = sem("xl_ready")
        g_done = sem("g_done")
        u_done = sem("u_done")
        sg_ready = sem("sg_ready")
        hf_ready = sem("hf_ready")
        hh_ready = sem("hh_ready")
        hl_ready = sem("hl_ready")
        d_done = sem("d_done")
        zz_ready = sem("zz_ready")
        oo_ready = sem("oo_ready")
        out_done = [sem(f"out_done{k}") for k in range(2)]

        block = ctx.enter_context(nc.Block())
        xview = X.rearrange("b (a t) d -> t a b d", t=P)
        oview = OUT.rearrange("b (a t) d -> t a b d", t=P)
        yview = y3_ap.rearrange("g p (a w) -> p a g w", w=W)

        @block.sync
        def _(sp):
            for par in range(2):
                sp.sem_inc(out_done[par], 16)

            def load(k, par):
                sp.dma_start(ya[:, par], yview[:, bass.ds(k, 1)].rearrange("p o g w -> p (o g) w")).then_inc(ya_in[par], 16)
                sp.dma_start(xr[:, par], xview[:, bass.ds(k, 1)].rearrange("p o b d -> p (o b) d")).then_inc(xr_in[par], 16)

            load(0, 0)
            sp.wait_ge(xr_in[0], 16)
            load(1, 1)
            sp.dma_start(wi[:, 2].rearrange("p (k h) -> p k h", k=HM), WDT).then_inc(w_in[2], 16)
            for k in range(3):
                sp.wait_ge(x1_ready, k + 1)
                load(k + 2, k % 2)

            def store(k, par):
                sp.wait_ge(oo_ready, k * NB + NB + 1)
                sp.dma_start(oview[:, bass.ds(k, 1)].rearrange("p o b d -> p (o b) d"), oo[:, par]).then_inc(out_done[par], 16)

            with sp.Fori(0, NA // 2 - 3) as kk:
                for par in range(2):
                    k = kk * 2 + par
                    sp.wait_ge(x1_ready, k + 4)
                    load(k + 5, 1 - par)
                    store(k, par)
            for k in range(NA - 6, NA):
                if k + 5 < NA:
                    sp.wait_ge(x1_ready, k + 4)
                    load(k + 5, 1 - k % 2)
                store(k, k % 2)
            sp.wait_ge(out_done[0], (NA // 2 + 1) * 16)
            sp.wait_ge(out_done[1], (NA // 2 + 1) * 16)

        def rounds(fori, body):
            with fori(0, 2) as q:
                for r in range(1, 7):
                    body(q * 6 + r, r % 2, r % 3)
            for k in range(13, NA):
                body(k, k % 2, k % 3)

        def ahead(k, d):
            return not isinstance(k, int) or k + d < NA

        def first(k):
            return isinstance(k, int) and k == 0

        def add_x(eng, r2):
            eng.tensor_tensor(x1[:, r2].rearrange("p b (g c) -> p b g c", g=NG),
                              ya[:, r2].rearrange("p g (c b) -> p b g c", b=NB),
                              xr[:, r2].rearrange("p b (g c) -> p b g c", g=NG), ALU.add).then_inc(x1_ready, 1)

        def count1(k):
            return 3 if first(k) else k * 2 + 2

        def count2(k):
            return k * 2 + 3 if ahead(k, 2) else NA + k

        @block.tensor
        def _(pe):
            def transposes(k, r3):
                pe.wait_ge(x1n_ready, k * NB + NB)
                if not first(k):
                    pe.wait_ge(xl_ready, k * KT)
                for t in range(KT):
                    for b in range(NB):
                        mm = pe.transpose(b_t[t][:, b * P:(b + 1) * P], x1n[:, r3, b, t * P:(t + 1) * P], ident[:])
                    mm.then_inc(tr_done, 1)

            def gate_up(k, r2, m):
                for wt, bk, free, done in ((wg, b_g, sg_ready, g_done), (wu, b_u, hf_ready, u_done)):
                    if m >= 2 or not first(k):
                        pe.wait_ge(free, k * HM + m - 1)
                    for t in range(KT):
                        for y in (xh, xl):
                            mm = pe.matmul(bk[m % 2][:, :], wt[:, t, m * P:(m + 1) * P], y[:, r2, t, :],
                                           start=(t == 0 and y is xh), stop=(t == KT - 1 and y is xl))
                    mm.then_inc(done, 1)

            def down(k, r2):
                pe.wait_ge(hh_ready, k * HM + HM)
                pe.wait_ge(hl_ready, k * HM + HM)
                pe.wait_ge(zz_ready, k * 2 + 1)
                for b in range(NB):
                    for m in range(HM):
                        for h in (hh, hl):
                            mm = pe.matmul(b_d[b // 2][:, (b % 2) * D:(b % 2 + 1) * D],
                                           h[:, r2, m, b * P:(b + 1) * P], wd[:, m, :],
                                           start=(m == 0 and h is hh), stop=(m == HM - 1 and h is hl))
                    if b % 2:
                        mm.then_inc(d_done, 1)

            def step(k, r2, r3):
                pe.wait_ge(xh_ready, k * KT + KT)
                pe.wait_ge(xl_ready, k * KT + KT)
                for m in range(HM):
                    gate_up(k, r2, m)
                    if m == 1:
                        if ahead(k, 1):
                            transposes(k + 1, (r3 + 1) % 3)
                        if not first(k):
                            down(k - 1, 1 - r2)

            pe.wait_ge(id_in, 16)
            transposes(0, 0)
            pe.wait_ge(w_cast, 2)
            step(0, 0, 0)
            pe.wait_ge(w_cast, 3)
            rounds(pe.Fori, step)
            down(NA - 1, (NA - 1) % 2)

        @block.scalar
        def _(act):
            def split_x(k, par):
                act.wait_ge(tr_done, k * KT + KT)
                for t in range(KT):
                    nc.scalar.activation(xh[:, par, t, :], b_t[t][:, :], ACT.Copy, scale=XS).then_inc(xh_ready, 1)

            def silu(k, m):
                act.wait_ge(g_done, k * HM + m + 1)
                if m >= 3 or not first(k):
                    act.wait_ge(hf_ready, k * HM + m - 2)
                nc.scalar.activation(sg[:, m % 3, :], b_g[m % 2][:, :], ACT.Silu, scale=QS / XS).then_inc(sg_ready, 1)

            def high(k, r2, m):
                act.wait_ge(hf_ready, k * HM + m + 1)
                nc.scalar.activation(hh[:, r2, m, :], hf[:, m % 3, :], ACT.Copy).then_inc(hh_ready, 1)

            def step(k, r2, r3):
                silu(k, 0)
                silu(k, 1)
                high(k, r2, 0)
                if ahead(k, 1):
                    split_x(k + 1, 1 - r2)
                high(k, r2, 1)
                silu(k, 2)
                for m in range(3, HM):
                    silu(k, m)
                    high(k, r2, m - 1)
                high(k, r2, HM - 1)

            act.dma_start(ident[:], IDENT).then_inc(id_in, 16)
            act.wait_ge(xr_in[0], 16)
            act.dma_start(wi[:, 0].rearrange("p (k h) -> p k h", k=KT), WGT).then_inc(w_in[0], 16)
            act.dma_start(wi[:, 1].rearrange("p (k h) -> p k h", k=KT), WUT).then_inc(w_in[1], 16)
            for q in range(3):
                if q == 1:
                    split_x(0, 0)
                act.wait_ge(w_in[q], 16)
                nc.scalar.activation(wq[:, q], wi[:, q], ACT.Copy).then_inc(w_cast, 1)
            step(0, 0, 0)
            rounds(act.Fori, step)

        @block.vector
        def _(dve):
            def row_stats(src, slot, count):
                for b in range(NB):
                    last = nc.vector.bn_stats(st[:, slot, b, :], src[:, b, :])
                last.then_inc(stats, 1)
                dve.wait_ge(stats, count)
                nc.vector.memset(tick[:], 0.0)
                for b in range(NB):
                    last = nc.vector.bn_aggr(mv[:, slot, b, :], st[:, slot, b, :])
                last.then_inc(mean_ready, 1)

            def normalise(dst, src, slot, count, done):
                dve.wait_ge(rstd, count)
                for b in range(NB):
                    nc.vector.tensor_scalar(dst[:, b, :], src[:, b, :], mv[:, slot, b, 0:1], rs[:, slot, b:b + 1],
                                            ALU.subtract, ALU.mult).then_inc(done, 1)

            def stats1(k, r2, count):
                dve.wait_ge(x1_ready, k + 1)
                row_stats(x1[:, r2], 0, count)

            def norm1(k, r2, r3, count):
                normalise(x1n[:, r3], x1[:, r2], 0, count, x1n_ready)

            def split_x(k, r2):
                for t in range(KT):
                    dve.wait_ge(xh_ready, k * KT + t + 1)
                    nc.vector.scalar_tensor_tensor(out=xl[:, r2, t, :], in0=b_t[t][:, :], scalar=XS,
                                                   in1=xh[:, r2, t, :], op0=ALU.mult,
                                                   op1=ALU.subtract).then_inc(xl_ready, 1)

            def product(k, m):
                dve.wait_ge(u_done, k * HM + m + 1)
                dve.wait_ge(sg_ready, k * HM + m + 1)
                if m >= 3 or not first(k):
                    dve.wait_ge(hl_ready, k * HM + m - 2)
                nc.vector.scalar_tensor_tensor(out=hf[:, m % 3, :], in0=b_u[m % 2][:, :], scalar=HS * QS / XS,
                                               in1=sg[:, m % 3, :], op0=ALU.mult,
                                               op1=ALU.mult).then_inc(hf_ready, 1)

            def sum2(k, r3):
                dve.wait_ge(oo_ready, k * NB + 1)
                for h in range(2):
                    dve.wait_ge(d_done, k * 2 + h + 1)
                    nc.vector.scalar_tensor_tensor(
                        out=zz[:, 2 * h:2 * h + 2, :], in0=b_d[h][:, :].rearrange("p (b c) -> p b c", b=2),
                        scalar=QS / HS, in1=x1n[:, r3, 2 * h:2 * h + 2, :], op0=ALU.mult,
                        op1=ALU.add).then_inc(zz_ready, 1)

            def stats2(k, count):
                dve.wait_ge(zz_ready, k * 2 + 2 + 1)
                row_stats(zz, 1, count)

            def norm2(k, r2, free, count):
                dve.wait_ge(out_done[r2], free)
                normalise(oo[:, r2], zz, 1, count, oo_ready)

            def step(k, r2, r3):
                free = 0 if first(k) else ((k - 1 - (1 - r2)) * 8 + 16)
                product(k, 0)
                product(k, 1)
                if ahead(k, 1):
                    split_x(k + 1, 1 - r2)
                if ahead(k, 2):
                    stats1(k + 2, r2, count1(k))
                if not first(k):
                    sum2(k - 1, (r3 + 2) % 3)
                product(k, 2)
                if ahead(k, 2):
                    if not first(k):
                        dve.wait_ge(zz_ready, k * 2 + 1)
                    norm1(k + 2, r2, (r3 + 2) % 3, count1(k))
                product(k, 3)
                if not first(k):
                    stats2(k - 1, count2(k))
                product(k, 4)
                product(k, 5)
                if not first(k):
                    norm2(k - 1, 1 - r2, free, count2(k))

            nc.vector.memset(epst[:], EPS)
            nc.vector.memset(mhalf[:], -0.5).then_inc(const_ready, 1)
            dve.sem_inc(zz_ready, 1)
            dve.sem_inc(oo_ready, 1)
            for k in range(2):
                dve.wait_ge(ya_in[k], 16)
                dve.wait_ge(xr_in[k], 16)
                add_x(nc.vector, k)
                stats1(k, k, k + 1)
                norm1(k, k, k, k + 1)
                if k == 0:
                    split_x(0, 0)
            step(0, 0, 0)
            rounds(dve.Fori, step)
            sum2(NA - 1, (NA - 1) % 3)
            stats2(NA - 1, 2 * NA)
            norm2(NA - 1, 1, NA // 2 * 16, 2 * NA)

        @block.gpsimd
        def _(pool):
            def add(k, r2):
                pool.wait_ge(ya_in[r2], (k - r2) * 8 + 16)
                pool.wait_ge(xr_in[r2], (k - r2) * 8 + 16)
                add_x(nc.gpsimd, r2)

            def root(slot, count):
                pool.wait_ge(mean_ready, count)
                nc.gpsimd.tensor_tensor(rs[:, slot], mv[:, slot, :, 1], epst[:], ALU.add).then_inc(var_ready, 1)
                pool.wait_ge(var_ready, count)
                nc.gpsimd.tensor_tensor(rs[:, slot], rs[:, slot], mhalf[:], ALU.pow).then_inc(rstd, 1)

            def low(k, r2, m):
                pool.wait_ge(hh_ready, k * HM + m + 1)
                nc.gpsimd.tensor_tensor(hl[:, r2, m, :], hf[:, m % 3, :], hh[:, r2, m, :],
                                        ALU.subtract).then_inc(hl_ready, 1)

            def step(k, r2, r3):
                low(k, r2, 0)
                low(k, r2, 1)
                if ahead(k, 2):
                    root(0, count1(k))
                if ahead(k, 3):
                    pool.wait_ge(x1n_ready, k * NB + 2 * NB)
                    add(k + 3, 1 - r2)
                low(k, r2, 2)
                low(k, r2, 3)
                if not first(k):
                    root(1, count2(k))
                low(k, r2, 4)
                low(k, r2, 5)

            pool.wait_ge(const_ready, 1)
            root(0, 1)
            root(0, 2)
            pool.wait_ge(x1n_ready, NB)
            add(2, 0)
            step(0, 0, 0)
            rounds(pool.Fori, step)
            root(1, 2 * NA)


def tables():
    k = np.arange(P)
    period = np.power(np.float32(10000.0), (2 * k).astype(np.float32) / np.float32(D)).astype(np.float32)
    t = np.arange(T)
    lag_angle = (t[:P, None].astype(np.float32) / period[None, :]).astype(np.float32).astype(np.float64)
    angle = t[:, None].astype(np.float64) / period[None, :].astype(np.float64)
    sin, cos = np.sin(angle), np.cos(angle)
    posr = np.stack([np.sin(lag_angle).T, np.cos(lag_angle).T], 1).astype(np.float32)
    high = [x.astype(np.float16) for x in (cos, sin)]
    low = [(x - h.astype(np.float64)).astype(np.float16) for x, h in zip((cos, sin), high)]
    ef = np.stack(high + low, 0).reshape(4, NA, P, P)[:, :NA - 1].transpose(2, 1, 0, 3)
    ei = np.stack([sin.T, cos.T], 1).astype(np.float32)
    row = np.arange(P)
    step = np.zeros((P, NA - 1, P // 2), np.float16)
    sel = np.zeros((P // 2, NA, P), np.float16)
    for a in range(NA):
        if a < NA - 1:
            step[:, a, (row[:P // 2] % 32 < NA) & (row[:P // 2] % 32 > a)] = 1
        sel[[a, 32 + a], a, :] = 1 / BSC
    flip = (np.eye(P)[::-1]).astype(np.float16)
    return posr[:, :, ::-1], np.ascontiguousarray(ef), ei, step, sel, flip


def kernel(L0_attn_X, L0_attn_Wp, L0_attn_bp, L0_attn_Wf, L0_attn_bf, L0_ffn_w_gate, L0_ffn_w_up, L0_ffn_w_down):
    import concourse.bacc as bacc
    from concourse.bass_utils import run_bass_kernel_spmd

    X = np.asarray(L0_attn_X)
    posr, ef, ei, step, sel, flip = tables()

    def by_group(w):
        return w.reshape(w.shape[:-1] + (NS + 1, NG, CG)).swapaxes(-3, -2).reshape(w.shape[:-1] + (NG, (NS + 1) * CG))

    wf = np.asarray(L0_attn_Wf)
    bf = np.asarray(L0_attn_bf)
    wpg = by_group(np.asarray(L0_attn_Wp)).reshape(KT, P, NG, (NS + 1) * CG).transpose(2, 1, 0, 3)
    arrays = {
        "XT": X.reshape(NB, NA, P, KT, P).transpose(4, 3, 1, 0, 2),
        "X": X,
        "WPG": np.concatenate([wpg, wpg[:1]]),
        "BPG": by_group(np.asarray(L0_attn_bp)),
        "WF": np.stack([wf[0::2], wf[1::2]], 1),
        "BFC": bf.reshape(NS * D // P, P).T,
        "BFR": bf,
        "POSR": posr, "EF": ef, "EI": ei, "STEP": step, "SEL": sel, "FLIP": flip,
        "ONES": np.ones((P, P), np.float32), "IDENT": np.eye(P, dtype=np.float32),
        "WGT": np.asarray(L0_ffn_w_gate).T.reshape(KT, P, HID).transpose(1, 0, 2),
        "WUT": np.asarray(L0_ffn_w_up).T.reshape(KT, P, HID).transpose(1, 0, 2),
        "WDT": np.asarray(L0_ffn_w_down).T.reshape(HM, P, D).transpose(1, 0, 2),
    }
    nc = bacc.Bacc("TRN2", target_bir_lowering=False, num_devices=1)
    ins, args = {}, []
    for name, a in arrays.items():
        ins[f"in_{name}"] = np.ascontiguousarray(a)
        args.append(nc.dram_tensor(f"in_{name}", a.shape, mybir.dt.from_np(a.dtype), kind="ExternalInput").ap())
    args.append(nc.dram_tensor("out_x", [NB, T, D], F32, kind="ExternalOutput").ap())
    program(nc, *args)
    r = run_bass_kernel_spmd(nc, [ins], core_ids=[0])
    return r.results[0]["out_x"]
```
